# Optimizing a Trainium2 kernel written in Bass

```python
import numpy as np
import jax
import jax.numpy as jnp

def _softmax(x, axis=-1):
    return jax.nn.softmax(x, axis=axis)

def _gelu(x):
    return jax.nn.gelu(x, approximate=True)

def _silu(x):
    return jax.nn.silu(x)

def _sigmoid(x):
    return jax.nn.sigmoid(x)

def _layernorm(x, axis=-1, eps=1e-05):
    m = jnp.mean(x, axis=axis, keepdims=True)
    v = jnp.var(x, axis=axis, keepdims=True)
    return (x - m) / jnp.sqrt(v + eps)

def _scatter_add(tgt, idx, src, axis=0):
    return tgt.at[idx].add(src)

def _segment_sum(src, seg, n):
    return jax.ops.segment_sum(src, seg, n)
kernel_name = 'mk_xattn_ffn_d1_seqx_r8_c86f24'

def setup_inputs(seed: int=0):
    np.random.seed(seed)
    _w = jnp.asarray

    def _rec_inputs():
        import jax
        import jax.numpy as jnp
        _rk = jax.random.key(seed)
        x = 7.22e-05 + 1 * jax.random.normal(jax.random.fold_in(_rk, 1), (16, 128, 256), jnp.float32)
        _lenS = 128 - jax.random.randint(jax.random.fold_in(_rk, 7), (16,), 0, max(1, 128 // 4) + 1, jnp.int32)
        _lenS2 = 128 - jax.random.randint(jax.random.fold_in(_rk, 8), (16,), 0, max(1, 128 // 4) + 1, jnp.int32)
        _ctx_1024P = jax.random.normal(jax.random.fold_in(_rk, 11), (16, 16, 128), jnp.float32)
        _ctx_1024c = jax.random.dirichlet(jax.random.fold_in(_rk, 511), 0.3 * jnp.ones((16,), jnp.float32), (16, 128))
        _ctx_1024t = jnp.einsum('bsk,bkd->bsd', _ctx_1024c, _ctx_1024P)
        _ctx_1024t = _ctx_1024t * jax.lax.rsqrt(jnp.mean(jnp.square(_ctx_1024t)) + 1e-12) * 0.953939
        ctx_1024 = -1.39393e-06 + 0.999914 * (_ctx_1024t + 0.3 * jax.random.normal(jax.random.fold_in(_rk, 611), (16, 128, 128), jnp.float32))
        fside_BxSx2_0 = jax.random.uniform(jax.random.fold_in(_rk, 12), (16, 128, 2), jnp.float32, 0.0, 0.999707)
        return (x, ctx_1024, fside_BxSx2_0)
    x, ctx_1024, fside_BxSx2_0 = _rec_inputs()

    def _L0_xattn_setup():
        import jax, jax.numpy as jnp
        import numpy as np
        DIM = 256
        CTX_DIM = 128
        N_HEADS = 32
        HEAD_DIM = DIM // N_HEADS
        POS_DIM = 2
        B, N, CTXN = (2, 256, 256)
        ROPE_BASE = 10000.0

        def apply_axial_rope(x, pos):
            b, n, h, d = x.shape
            p = pos.shape[-1]
            dpa = d // p
            half = dpa // 2
            freqs = ROPE_BASE ** (-jnp.arange(half, dtype=x.dtype) / half)
            ang = pos[..., :, None] * freqs
            cos = jnp.cos(ang)[:, :, None, :, :]
            sin = jnp.sin(ang)[:, :, None, :, :]
            xr = x.reshape(b, n, h, p, half, 2)
            x1, x2 = (xr[..., 0], xr[..., 1])
            out = jnp.stack([x1 * cos - x2 * sin, x1 * sin + x2 * cos], axis=-1)
            return out.reshape(b, n, h, d)
        key = jax.random.key(seed)
        ks = jax.random.split(key, 8)
        x = jax.random.normal(ks[0], (B, N, DIM), jnp.float32)
        ctx = jax.random.normal(ks[1], (B, CTXN, CTX_DIM), jnp.float32)
        pos_map = jax.random.uniform(ks[2], (B, N, POS_DIM), jnp.float32)
        ctx_pos_map = jax.random.uniform(ks[3], (B, CTXN, POS_DIM), jnp.float32)
        Wq = jax.random.normal(ks[4], (DIM, DIM), jnp.float32) / np.sqrt(DIM)
        Wkv = jax.random.normal(ks[5], (CTX_DIM, 2 * DIM), jnp.float32) / np.sqrt(CTX_DIM)
        Wout = jax.random.normal(ks[6], (DIM, DIM), jnp.float32) / np.sqrt(DIM)
        bout = jnp.zeros((DIM,), jnp.float32)
        return {'x': x, 'ctx': ctx, 'pos_map': pos_map, 'ctx_pos_map': ctx_pos_map, 'Wq': Wq, 'Wkv': Wkv, 'Wout': Wout, 'bout': bout}
    _L0_xattn_all = _L0_xattn_setup()
    _L0_xattn_in = {k: v for k, v in _L0_xattn_all.items() if k in ('Wq', 'Wkv', 'Wout', 'bout')}
    del _L0_xattn_all

    def _L0_ffn_setup():
        import jax, jax.numpy as jnp
        import numpy as np
        B, S, D, F, E, K = (2, 256, 256, 1024, 8, 2)
        key = jax.random.key(seed)
        k0, k1, k2, k3 = jax.random.split(key, 4)
        scale = lambda k, shape, fan_in: jax.random.normal(k, shape, jnp.float32) * fan_in ** (-0.5)
        return {'inputs': jax.random.normal(k0, (B, S, D), jnp.float32), 'gate_w': scale(k1, (D, E), D), 'gate_b': jnp.zeros((E,), jnp.float32), 'w1': scale(k2, (E, D, F), D), 'b1': jnp.zeros((E, F), jnp.float32), 'w2': scale(k3, (E, F, D), F), 'b2': jnp.zeros((E, D), jnp.float32)}
    _L0_ffn_all = _L0_ffn_setup()
    _L0_ffn_in = {k: v for k, v in _L0_ffn_all.items() if k in ('gate_w', 'gate_b', 'w1', 'b1', 'w2', 'b2')}
    del _L0_ffn_all
    return {'x': x, 'ctx_1024': ctx_1024, 'fside_BxSx2_0': fside_BxSx2_0, 'L0_xattn_Wq': _L0_xattn_in['Wq'], 'L0_xattn_Wkv': _L0_xattn_in['Wkv'], 'L0_xattn_Wout': _L0_xattn_in['Wout'], 'L0_xattn_bout': _L0_xattn_in['bout'], 'L0_ffn_gate_w': _L0_ffn_in['gate_w'], 'L0_ffn_gate_b': _L0_ffn_in['gate_b'], 'L0_ffn_w1': _L0_ffn_in['w1'], 'L0_ffn_b1': _L0_ffn_in['b1'], 'L0_ffn_w2': _L0_ffn_in['w2'], 'L0_ffn_b2': _L0_ffn_in['b2']}

def reference(x, ctx_1024, fside_BxSx2_0, L0_xattn_Wq, L0_xattn_Wkv, L0_xattn_Wout, L0_xattn_bout, L0_ffn_gate_w, L0_ffn_gate_b, L0_ffn_w1, L0_ffn_b1, L0_ffn_w2, L0_ffn_b2):
    import jax
    import jax.numpy as jnp

    def _L0_xattn_ref(x, ctx, pos_map, ctx_pos_map, Wq, Wkv, Wout, bout):
        import jax, jax.numpy as jnp
        import numpy as np
        DIM = 256
        CTX_DIM = 128
        N_HEADS = 32
        HEAD_DIM = DIM // N_HEADS
        POS_DIM = 2
        B, N, CTXN = (2, 256, 256)
        ROPE_BASE = 10000.0

        def apply_axial_rope(x, pos):
            b, n, h, d = x.shape
            p = pos.shape[-1]
            dpa = d // p
            half = dpa // 2
            freqs = ROPE_BASE ** (-jnp.arange(half, dtype=x.dtype) / half)
            ang = pos[..., :, None] * freqs
            cos = jnp.cos(ang)[:, :, None, :, :]
            sin = jnp.sin(ang)[:, :, None, :, :]
            xr = x.reshape(b, n, h, p, half, 2)
            x1, x2 = (xr[..., 0], xr[..., 1])
            out = jnp.stack([x1 * cos - x2 * sin, x1 * sin + x2 * cos], axis=-1)
            return out.reshape(b, n, h, d)
        b, n, _ = x.shape
        ctx_n = ctx.shape[1]
        q = (x @ Wq).reshape(b, n, N_HEADS, HEAD_DIM)
        k, v = jnp.split(ctx @ Wkv, 2, axis=-1)
        k = k.reshape(b, ctx_n, N_HEADS, HEAD_DIM)
        v = v.reshape(b, ctx_n, N_HEADS, HEAD_DIM)
        q = apply_axial_rope(q, pos_map)
        k = apply_axial_rope(k, ctx_pos_map)
        scale = 1.0 / np.sqrt(HEAD_DIM).astype(np.float32)
        logits = jnp.einsum('bqhd,bkhd->bhqk', q, k) * scale
        w = jax.nn.softmax(logits, axis=-1)
        attn = jnp.einsum('bhqk,bkhd->bqhd', w, v)
        attn = attn.reshape(b, n, N_HEADS * HEAD_DIM)
        return attn @ Wout + bout

    def _L0_ffn_ref(inputs, gate_w, gate_b, w1, b1, w2, b2):
        import jax, jax.numpy as jnp
        import numpy as np
        B, S, D, F, E, K = (2, 256, 256, 1024, 8, 2)
        x = inputs.reshape(-1, inputs.shape[-1])
        n = x.shape[0]
        gate_probs = jax.nn.softmax(x @ gate_w + gate_b, axis=-1)
        weights, selected = jax.lax.top_k(gate_probs, K)
        weights = weights / jnp.sum(weights, axis=-1, keepdims=True)
        comb = jnp.zeros((n, E), x.dtype).at[jnp.arange(n)[:, None], selected].set(weights)
        h = jax.nn.gelu(jnp.einsum('nd,edf->enf', x, w1) + b1[:, None, :])
        expert_out = jnp.einsum('enf,efd->end', h, w2) + b2[:, None, :]
        out = jnp.einsum('ne,end->nd', comb, expert_out)
        return out.reshape(inputs.shape[:-1] + (out.shape[-1],))
    x = x + _L0_xattn_ref(_layernorm(x, axis=-1), ctx_1024, fside_BxSx2_0, fside_BxSx2_0, L0_xattn_Wq, L0_xattn_Wkv, L0_xattn_Wout, L0_xattn_bout)
    x = x + _L0_ffn_ref(_layernorm(x, axis=-1), L0_ffn_gate_w, L0_ffn_gate_b, L0_ffn_w1, L0_ffn_b1, L0_ffn_w2, L0_ffn_b2)
    return x

_drawn_inputs = setup_inputs


def setup_inputs(seed=0):
    import zlib

    import numpy as np

    out = dict(_drawn_inputs(seed))
    spreads = {'L0_xattn_bout': (0.0, 0.1),
     'L0_ffn_gate_b': (0.0, 0.1),
     'L0_ffn_b1': (0.0, 0.1),
     'L0_ffn_b2': (0.0, 0.1)}
    factors = {}
    for name, (base, spread) in spreads.items():
        noise = np.random.default_rng([zlib.crc32(name.encode()), seed]).standard_normal(out[name].shape)
        drawn = base * np.exp(spread * noise) if base else spread * noise
        out[name] = jnp.asarray(drawn.astype(out[name].dtype))
    for name, factor in factors.items():
        out[name] = (out[name] * factor).astype(out[name].dtype)
    return out
```

```python
from contextlib import ExitStack
import math

import numpy as np
import concourse.bass as bass
from concourse import mybir

F32 = mybir.dt.float32
F16 = mybir.dt.float16
I32 = mybir.dt.int32
ALU = mybir.AluOpType
ACT = mybir.ActivationFunctionType
AX = mybir.AxisListType

P = 128
B = 16
D = 256
DC = D // P
CD = 128
H = 32
HD = D // H
SLOT = 32
ROWT = P // SLOT
HG = H // ROWT
UNITS = 8
UH = H // UNITS
VW = HD + 1
NPB = 4
E = 8
F = 1024
FC = F // P
EPS = 1e-5
QS = 64.0
XS = 64.0
WS = 256.0
MROW = 3 * HD
EXP_SCALE = 1.0 / (QS * QS * math.sqrt(HD))
TWO_PI = 2.0 * math.pi
TILES = 2 * B + E - 1
RSQRT_OPS = 15
RSQRT_MAGIC = float(0x5F3759DF)


def count(b, per, k=None):
    return b * per + (per if k is None else k)


def rsqrt(eng, var, y, t, ti, done, base):
    n = [0]

    def chain(ins):
        n[0] += 1
        ins.then_inc(done, 1)
        eng.wait_ge(done, base + n[0])

    chain(eng.tensor_scalar(t[:, 0], var, EPS, None, ALU.add))
    chain(eng.tensor_copy(t[:, 1], t[:, 0].bitcast(I32)))
    chain(eng.tensor_scalar(ti, t[:, 1], -0.5, RSQRT_MAGIC, ALU.mult, ALU.add))
    guess = ti.bitcast(F32)
    for i in range(3):
        y_in = guess if i == 0 else y
        chain(eng.tensor_tensor(t[:, 1], y_in, y_in, ALU.mult))
        chain(eng.tensor_tensor(t[:, 2], t[:, 1], t[:, 0], ALU.mult))
        chain(eng.tensor_scalar(t[:, 2], t[:, 2], -0.5, 1.5, ALU.mult, ALU.add))
        chain(eng.tensor_tensor(y, y_in, t[:, 2], ALU.mult))


def build(nc, x, ctx_in, pos, wq, wkv, wout, bout, gate_w, gate_b, w1, b1, w2, b2, out):
    with ExitStack() as ctx:
        def sb(name, shape, dt):
            return ctx.enter_context(nc.sbuf_tensor(name, shape, dt))

        x1 = sb("x1", [P, B * D], F32)
        logits = sb("logits", [P, B, E], F32)
        w1h = sb("w1h", [P, E * DC * F], F16)
        w1l = sb("w1l", [P, E * DC * F], F16)
        w2h = sb("w2h", [P, E * FC * D], F16)
        w2l = sb("w2l", [P, E * FC * D], F16)
        ident = sb("ident", [P, P], F32)
        ident16 = sb("ident16", [P, P], F16)

        x2_dram = nc.dram_tensor("x2_dram", (B * P, 2 * D), F16, kind="Internal").ap()
        ids_dram = nc.dram_tensor("ids_dram", (TILES * P, 1), I32, kind="Internal").ap()
        y_dram = nc.dram_tensor("y_dram", (TILES * P, D), F32, kind="Internal").ap()

        attention(nc, x, ctx_in, pos, wq, wkv, wout, bout, gate_w, gate_b, w1, w2,
                  x1, logits, w1h, w1l, w2h, w2l, ident, ident16, x2_dram, ids_dram)
        experts(nc, b1, b2, out, x1, logits, w1h, w1l, w2h, w2l, ident, ident16, x2_dram, ids_dram, y_dram)


def attention(nc, x, ctx_in, pos, wq, wkv, wout, bout, gate_w, gate_b, w1, w2,
              x1, logits, w1h, w1l, w2h, w2l, ident, ident16, x2_dram, ids_dram):
    w1_chunks = w1.rearrange("e (k p) f -> (e k) p f", p=P)
    w2_chunks = w2.rearrange("e (h c p) d -> (e h) p c d", p=P, h=2)

    with ExitStack() as ctx:
        def sb(name, shape, dt):
            return ctx.enter_context(nc.sbuf_tensor(name, shape, dt))

        def bank(name, shape, dt):
            return ctx.enter_context(nc.psum_tensor(name, shape, dt))

        def sem(name):
            return ctx.enter_context(nc.semaphore(name))

        wq_sb = sb("wq_sb", [P, DC, D], F32)
        wkv_sb = sb("wkv_sb", [P, 2 * D], F32)
        wout_sb = sb("wout_sb", [P, DC, D], F32)
        zero_ids = sb("zero_ids", [TILES, P], I32)
        ws_sb = sb("ws_sb", [P, 1], F32)
        bout_bc = sb("bout_bc", [P, D], F32)
        gw_sb = sb("gw_sb", [P, DC, E], F32)
        gb_bc = sb("gb_bc", [P, E], F32)
        pos_sb = sb("pos_sb", [P, B, 2], F32)
        ang = sb("ang", [P, 2, B * 4], F32)
        turns = sb("turns", [P, 2, B * 4], F32)
        turns_i = sb("turns_i", [P, 2, B * 4], I32)
        sincos = sb("sincos", [P, 2, B * 4], F32)
        cos8 = sb("cos8", [P, B * HD], F32)
        sin8 = sb("sin8", [P, B * HD], F32)
        bn1 = sb("bn1", [P, 6], F32)
        mv1 = sb("mv1", [P, B * 2], F32)
        rs1 = sb("rs1", [P, B], F32)
        nt1 = sb("nt1", [P, 3, B], F32)
        nt1i = sb("nt1i", [P, B], I32)
        bn2 = sb("bn2", [P, 6], F32)
        st2 = sb("st2", [P, 4], F32)
        mv2 = sb("mv2", [P, 2], F32)
        rs2 = sb("rs2", [P, 1], F32)
        nt2 = sb("nt2", [P, 3, 1], F32)
        nt2i = sb("nt2i", [P, 1], I32)
        ctx_sb = sb("ctx_sb", [P, 2, CD], F32)
        xhat = sb("xhat", [P, D], F32)
        xT = sb("xT", [P, 3, P], F32)
        qk = sb("qk", [P, 2, D], F32)
        qkc = sb("qkc", [P, 2, D], F32)
        qks = sb("qks", [P, 2, D], F32)
        qx = [sb(f"qx{i}", [P, H, SLOT], F16) for i in range(2)]
        kx = sb("kx", [P, H, SLOT], F16)
        qT = [sb(f"qT{i}", [P, HG, P], F16) for i in range(2)]
        kT = [sb(f"kT{i}", [P, HG, P], F16) for i in range(2)]
        v = [sb(f"v{i}", [P, H, VW], F32) for i in range(2)]
        mx = sb("mx", [P, H], F32)
        probs = [sb(f"probs{i}", [P, UH * P], F32) for i in range(NPB)]
        recip = sb("recip", [P, H], F32)
        attn = sb("attn", [P, D], F32)
        attnT = sb("attnT", [P, DC, P], F32)
        x1b = sb("x1b", [P, D], F32)
        x2f = sb("x2f", [P, D], F32)
        x2 = sb("x2", [P, 2, 2 * D], F16)
        x2T = sb("x2T", [P, DC, P], F32)
        w1_stage = sb("w1_stage", [P, F], F32)
        w2_stage = sb("w2_stage", [P, F], F32)

        s_bank = [bank(f"s_bank{i}", [P, 512], F32) for i in range(2)]
        t_bank = [bank(f"t_bank{i}", [P, 512], F32) for i in range(2)]
        av_bank = bank("av_bank", [P, H, 16], F32)
        m0 = bank("m0", [P, 512], F32)
        m1 = bank("m1", [P, 512], F32)
        m2 = bank("m2", [P, 512], F32)
        m0_16 = m0[:, :].bitcast(F16)
        m1_16 = m1[:, :].bitcast(F16)

        names = """consts_ready setup_v setup_a setup_p x_loaded pos_loaded small_loaded
        w1_loaded w2_loaded tables_ready slots_ready
        pe_xT pe_q pe_kv pe_tk pe_tq1 pe_tq2 pe_s pe_st pe_av pe_attnT pe_out pe_x2T pe_gate
        act_xT act_qk act_v act_hi act_exp act_attnT act_x2hi act_x2T act_w
        dve_max dve_m dve_tk dve_tq1 dve_tq2 dve_rec dve_norm dve_x1 dve_bn dve_stats dve_gate
        dve_xhat pool_xb pool_mul pool_rope pool_lo dve_chain dve_x2 pool_x2lo pool_ws pool_w
        stored""".split()
        sems = {n: sem(n) for n in names}
        (consts_ready, setup_v, setup_a, setup_p, x_loaded, pos_loaded, small_loaded,
         w1_loaded, w2_loaded, tables_ready, slots_ready,
         pe_xT, pe_q, pe_kv, pe_tk, pe_tq1, pe_tq2, pe_s, pe_st, pe_av, pe_attnT, pe_out, pe_x2T, pe_gate,
         act_xT, act_qk, act_v, act_hi, act_exp, act_attnT, act_x2hi, act_x2T, act_w,
         dve_max, dve_m, dve_tk, dve_tq1, dve_tq2, dve_rec, dve_norm, dve_x1, dve_bn, dve_stats, dve_gate,
         dve_xhat, pool_xb, pool_mul, pool_rope, pool_lo, dve_chain, dve_x2, pool_x2lo, pool_ws, pool_w,
         stored) = [sems[n] for n in names]
        ctx_loaded = [sem(f"ctx_loaded{i}") for i in range(2)]
        x2_stored = [sem(f"x2_stored{i}") for i in range(2)]

        def paired(b, par):
            return 8 * b + (16 if par == 0 else 8)

        def run_steps(eng, step):
            for s in range(-1, 2):
                step(s, s % 2)
            with eng.Fori(1, B // 2 - 1) as pair:
                step(2 * pair, 0)
                step(2 * pair + 1, 1)
            for s in range(B - 2, B + 2):
                step(s, s % 2)

        def has(b):
            return not isinstance(b, int) or 0 <= b < B

        def peeled(s):
            return isinstance(s, int)

        block = ctx.enter_context(nc.Block())

        @block.sync
        def _(sp):
            sp.dma_start(pos_sb[:], pos.rearrange("b p c -> p b c")).then_inc(pos_loaded, 16)
            sp.dma_start(x1[:, :].rearrange("p (b d) -> p b d", b=B),
                         x.rearrange("b p d -> p b d")).then_inc(x_loaded, 16)
            sp.dma_start(wq_sb[:], wq.rearrange("(c p) n -> p c n", p=P)).then_inc(small_loaded, 16)
            sp.dma_start(wkv_sb[:], wkv).then_inc(small_loaded, 16)
            sp.dma_start(wout_sb[:], wout.rearrange("(c p) n -> p c n", p=P)).then_inc(small_loaded, 16)
            sp.dma_start(gw_sb[:], gate_w.rearrange("(c p) n -> p c n", p=P)).then_inc(small_loaded, 16)
            sp.dma_start(bout_bc[:], bout.rearrange("(a d) -> a d", a=1).to_broadcast([P, D])).then_inc(small_loaded, 16)
            sp.dma_start(gb_bc[:], gate_b.rearrange("(a d) -> a d", a=1).to_broadcast([P, E])).then_inc(small_loaded, 16)

            sp.wait_ge(slots_ready, 1)
            sp.dma_start(ids_dram.rearrange("(t p) a -> t (p a)", p=P), zero_ids[:]).then_inc(stored, 16)

            def step(s, par):
                if has(s + 2):
                    if not peeled(s) or s >= 0:
                        sp.wait_ge(pe_xT, count(s, 1))
                    sp.dma_start(ctx_sb[:, par, :], ctx_in[s + 2] if peeled(s) else ctx_in[bass.ds(s + 2, 1)].rearrange("a p c -> (a p) c")).then_inc(ctx_loaded[par], 16)
                if has(s + 1):
                    if has(s):
                        sp.wait_ge(act_w, count(s, 2))
                        sp.wait_ge(pool_ws, count(s, 4))
                    c = s + 1
                    one = w1_chunks[c] if peeled(s) else w1_chunks[bass.ds(c, 1)].rearrange("a p f -> (a p) f")
                    two = w2_chunks[c] if peeled(s) else w2_chunks[bass.ds(c, 1)].rearrange("a p c d -> (a p) c d")
                    sp.dma_start(w1_stage[:], one).then_inc(w1_loaded, 16)
                    sp.dma_start(w2_stage[:].rearrange("p (c d) -> p c d", d=D), two).then_inc(w2_loaded, 16)

                b = s - 2
                if has(b):
                    sp.wait_ge(pool_x2lo, count(b, 1))
                    sp.dma_start(x2_dram[bass.ds(b * P, P), :], x2[:, par, :]).then_inc(x2_stored[par], 16)

            sp.dma_start(ctx_sb[:, 0, :], ctx_in[0]).then_inc(ctx_loaded[0], 16)
            run_steps(sp, step)
            sp.wait_ge(stored, 16)
            for i in range(2):
                sp.wait_ge(x2_stored[i], 16 * (B // 2))

        @block.gpsimd
        def _(pool):
            pool.memset(ident[:], 0.0).then_inc(setup_p, 1)
            pool.wait_ge(setup_p, 1)
            pool.affine_select(out=ident[:], in_=ident[:], compare_op=ALU.not_equal, fill=1.0, base=0,
                               pattern=[[-1, P]], channel_multiplier=1).then_inc(setup_p, 1)
            pool.wait_ge(setup_p, 2)
            pool.memset(ws_sb[:], WS)
            pool.tensor_copy(ident16[:], ident[:]).then_inc(consts_ready, 1)
            ws_bc = ws_sb[:].to_broadcast([P, F])
            pool.memset(zero_ids[:], 0)
            pool.memset(qx[0][:], 0.0)
            pool.memset(qx[1][:], 0.0)
            pool.memset(kx[:], 0.0).then_inc(setup_p, 1)
            pool.memset(v[0][:], 1.0)
            pool.memset(v[1][:], 1.0)
            pool.wait_ge(setup_p, 3)
            pool.memset(kx[:, :, MROW], QS).then_inc(slots_ready, 1)

            def alone():
                pool.wait_ge(consts_ready, 1)

            def add_bias(b):
                pool.wait_ge(dve_xhat, count(b, 1))
                alone()
                xb = x1[:, bass.ds(b * D, D)]
                pool.tensor_tensor(xb, xb, bout_bc[:], ALU.add).then_inc(pool_xb, 1)

            def step(s, par):
                if has(s):
                    pool.wait_ge(w1_loaded, count(s, 16))
                    if peeled(s) and s == 0:
                        pool.wait_ge(consts_ready, 1)
                    pool.tensor_tensor(w1_stage[:], w1_stage[:], ws_bc, ALU.mult).then_inc(pool_ws, 1)
                    pool.wait_ge(w2_loaded, count(s, 16))
                    pool.tensor_tensor(w2_stage[:], w2_stage[:], ws_bc, ALU.mult).then_inc(pool_ws, 1)
                b = s + 1
                if has(b):
                    pool.wait_ge(act_qk, count(b, 1))
                    if peeled(b) and b == 0:
                        pool.wait_ge(tables_ready, 1)
                    if not peeled(b) or b >= 1:
                        pool.wait_ge(act_hi, count(b - 1, 1))
                    for i in range(2):
                        src = qk[:, i, :].rearrange("p (h d) -> p h d", d=HD)
                        for dst, table in ((qkc, cos8), (qks, sin8)):
                            tab = table[:, bass.ds(b * HD, HD)].rearrange("p (a d) -> p a d", a=1).to_broadcast([P, H, HD])
                            pool.tensor_tensor(dst[:, i, :].rearrange("p (h d) -> p h d", d=HD), src, tab,
                                               ALU.mult).then_inc(pool_mul, 1)
                    pool.wait_ge(pool_mul, count(b, 4))
                    pairs_c = qkc[:].rearrange("p i (n e) -> p (i n) e", e=2)
                    pairs_s = qks[:].rearrange("p i (n e) -> p (i n) e", e=2)
                    pool.tensor_tensor(pairs_c[:, :, 0], pairs_c[:, :, 0], pairs_s[:, :, 1], ALU.add)
                    pool.tensor_tensor(pairs_c[:, :, 1], pairs_c[:, :, 1], pairs_s[:, :, 0], ALU.add).then_inc(pool_rope, 1)
                b = s - 2
                if has(b):
                    pool.wait_ge(act_x2hi, count(b, 1))
                    pool.tensor_tensor(x2[:, par, D:2 * D], x2f[:], x2[:, par, 0:D],
                                       ALU.subtract).then_inc(pool_x2lo, 1)
                b = s + 1
                if has(b):
                    pool.wait_ge(act_hi, count(b, 1))
                    q4 = qx[1 - par][:].rearrange("p h (k d) -> p h k d", d=HD)
                    k4 = kx[:].rearrange("p h (k d) -> p h k d", d=HD)
                    pool.tensor_tensor(q4[:, :, 2, :], qkc[:, 0, :].rearrange("p (h d) -> p h d", d=HD), q4[:, :, 0, :],
                                       ALU.subtract)
                    pool.tensor_tensor(k4[:, :, 1, :], qkc[:, 1, :].rearrange("p (h d) -> p h d", d=HD), k4[:, :, 0, :],
                                       ALU.subtract).then_inc(pool_lo, 1)
                if has(s):
                    pool.wait_ge(act_w, count(s, 2, 1))
                    alone()
                    pool.tensor_tensor(w1l[:, bass.ds(s * F, F)], w1_stage[:], w1h[:, bass.ds(s * F, F)],
                                       ALU.subtract).then_inc(pool_ws, 1)
                    pool.wait_ge(act_w, count(s, 2))
                    alone()
                    pool.tensor_tensor(w2l[:, bass.ds(s * F, F)], w2_stage[:], w2h[:, bass.ds(s * F, F)],
                                       ALU.subtract).then_inc(pool_ws, 1)
                if has(s + 2):
                    add_bias(s + 2)

            pool.wait_ge(small_loaded, 16 * 6)
            add_bias(0)
            run_steps(pool, step)

        @block.scalar
        def _(act):
            act.wait_ge(setup_v, 12)
            act.activation(sincos[:], ang[:], ACT.Sin).then_inc(setup_a, 1)

            def exp_unit(b, u):
                act.wait_ge(pe_st, count(b, UNITS, u + 1))
                if not peeled(b) or b * UNITS + u >= NPB:
                    act.wait_ge(pe_av, count(b, UNITS, u + 1 - NPB))
                act.activation(probs[u % NPB][:], t_bank[u % 2][:], ACT.Exp, scale=EXP_SCALE).then_inc(act_exp, 1)

            def split_weights(s, k):
                stage, hi, ready = ((w1_stage, w1h, 1), (w2_stage, w2h, 2))[k]
                act.wait_ge(pool_ws, count(s, 4, ready))
                act.copy(hi[:, bass.ds(s * F, F)], stage[:]).then_inc(act_w, 1)

            def step(s, par):
                for u in range(UNITS):
                    if has(s - 1):
                        exp_unit(s - 1, u)
                    b = s + 1
                    if u == 0 and has(b):
                        act.wait_ge(pe_xT, count(b, 1))
                        if not peeled(b) or b >= 1:
                            act.wait_ge(pe_kv, count(b - 1, 1))
                        act.copy(xT[:], m0[:, 0:3 * P].rearrange("p (c t) -> p c t", c=3)).then_inc(act_xT, 1)
                    if u == 2 and has(b):
                        act.wait_ge(pe_q, count(b, 1))
                        if not peeled(b) or b >= 1:
                            act.wait_ge(pool_mul, count(b - 1, 4))
                        act.copy(qk[:, 0, :], m1[:, 0:D])
                        act.wait_ge(pe_kv, count(b, 1))
                        act.copy(qk[:, 1, :], m2[:, 0:D]).then_inc(act_qk, 1)
                    if u == 3 and has(s - 2):
                        c = s - 2
                        act.wait_ge(dve_x2, count(c, 1))
                        if not peeled(c) or c >= 2:
                            act.wait_ge(x2_stored[par], paired(c - 2, par))
                        act.copy(x2[:, par, 0:D], x2f[:]).then_inc(act_x2hi, 1)
                    if u == 4 and has(s):
                        split_weights(s, 0)
                    if u == 5 and has(s - 2):
                        c = s - 2
                        act.wait_ge(pe_x2T, count(c, 1))
                        if not peeled(c) or c >= 1:
                            act.wait_ge(pe_gate, count(c - 1, 1))
                        act.mul(x2T[:], m0[:, 0:D].rearrange("p (c t) -> p c t", c=DC), 1.0 / XS).then_inc(act_x2T, 1)
                    if u == 6 and has(b):
                        act.wait_ge(pool_rope, count(b, 1))
                        if peeled(b) and b == 0:
                            act.wait_ge(slots_ready, 1)
                        if not peeled(b) or b >= 1:
                            act.wait_ge(pe_tk, count(b - 1, 1))
                        if not peeled(b) or b >= 2:
                            act.wait_ge(pe_tq2, count(b - 2, 1))
                        q4 = qx[1 - par][:].rearrange("p h (k d) -> p h k d", d=HD)
                        k4 = kx[:].rearrange("p h (k d) -> p h k d", d=HD)
                        qr = qkc[:, 0, :].rearrange("p (h a d) -> p h a d", a=1, d=HD).to_broadcast([P, H, 2, HD])
                        kr = qkc[:, 1, :].rearrange("p (h a d) -> p h a d", a=1, d=HD).to_broadcast([P, H, 2, HD])
                        act.copy(q4[:, :, 0:2, :], qr)
                        act.copy(k4[:, :, 0:4:2, :], kr).then_inc(act_hi, 1)
                if has(s + 1):
                    b = s + 1
                    if not peeled(b) or b >= 2:
                        act.wait_ge(pe_av, count(b - 2, UNITS))
                    if peeled(b) and b == 0:
                        act.wait_ge(slots_ready, 1)
                    act.copy(v[1 - par][:, :, 0:HD], m2[:, D:2 * D].rearrange("p (h d) -> p h d", d=HD)).then_inc(act_v, 1)
                if has(s):
                    split_weights(s, 1)
                if has(s - 1):
                    c = s - 1
                    act.wait_ge(pe_attnT, count(c, 1))
                    if not peeled(c) or c >= 1:
                        act.wait_ge(pe_out, count(c - 1, 1))
                    act.copy(attnT[:], m2[:, 0:D].rearrange("p (c t) -> p c t", c=DC)).then_inc(act_attnT, 1)

            run_steps(act, step)

        @block.vector
        def _(dve):
            n = [0]

            def chain(ins):
                n[0] += 1
                ins.then_inc(setup_v, 1)
                dve.wait_ge(setup_v, n[0])

            dve.wait_ge(pos_loaded, 16)
            a4 = ang[:, 0, :].rearrange("p (n j) -> p n j", j=2)
            flat = pos_sb[:].rearrange("p b c -> p (b c)")
            for j in range(2):
                chain(dve.tensor_scalar(a4[:, :, j], flat, float(np.float32(10000.0 ** (-j / 2))), None, ALU.mult))
            chain(dve.tensor_scalar(ang[:, 1, :], ang[:, 0, :], math.pi / 2, None, ALU.add))
            chain(dve.tensor_scalar(turns_i[:], ang[:], 1.0 / TWO_PI, None, ALU.mult))
            chain(dve.tensor_copy(turns[:], turns_i[:]))
            chain(dve.scalar_tensor_tensor(ang[:], turns[:], -TWO_PI, ang[:], ALU.mult, ALU.add))
            for sign, cmp in ((-1.0, ALU.is_gt), (1.0, ALU.is_lt)):
                chain(dve.tensor_scalar(turns[:], ang[:], -sign * math.pi, sign * TWO_PI, cmp, ALU.mult))
                chain(dve.tensor_tensor(ang[:], ang[:], turns[:], ALU.add))
            chain(dve.tensor_scalar(ang[:], ang[:], math.pi, -math.pi, ALU.min, ALU.max))
            dve.wait_ge(x_loaded, 16)
            for b in range(B):
                chain(dve.bn_stats(bn1[:], x1[:, b * D:(b + 1) * D]))
                chain(dve.bn_aggr(mv1[:, b * 2:b * 2 + 2], bn1[:]))
            var1 = mv1[:].rearrange("p (b k) -> p b k", k=2)[:, :, 1]
            base = n[0]
            rsqrt(dve, var1, rs1[:], nt1, nt1i[:], setup_v, base)
            n[0] = base + RSQRT_OPS
            dve.wait_ge(setup_a, 1)
            c2 = cos8[:].rearrange("p (n e) -> p n e", e=2)
            s2 = sin8[:].rearrange("p (n e) -> p n e", e=2)
            dve.tensor_scalar(c2[:, :, 0], sincos[:, 1, :], QS, None, ALU.mult)
            dve.tensor_scalar(c2[:, :, 1], sincos[:, 1, :], QS, None, ALU.mult)
            dve.tensor_scalar(s2[:, :, 0], sincos[:, 0, :], QS, None, ALU.mult)
            dve.tensor_scalar(s2[:, :, 1], sincos[:, 0, :], -QS, None, ALU.mult).then_inc(tables_ready, 1)

            def normalize(b):
                dve.tensor_scalar(xhat[:], x1[:, bass.ds(b * D, D)], mv1[:, bass.ds(b * 2, 1)], rs1[:, bass.ds(b, 1)],
                                  ALU.subtract, ALU.mult).then_inc(dve_xhat, 1)

            def evacuate(dst, src, ready, done, b):
                dve.wait_ge(ready, count(b, 1))
                dve.tensor_copy(dst[:], src.rearrange("p (g t) -> p g t", g=HG)).then_inc(done, 1)

            mx_units = mx[:].rearrange("p (k g j) -> p k g j", k=2, j=ROWT)

            def step(s, par):
                for u in range(UNITS):
                    if has(s):
                        dve.wait_ge(pe_s, count(s, UNITS, u + 1))
                        if u == 0 and (not peeled(s) or s >= 1):
                            dve.wait_ge(dve_m, count(s - 1, 1))
                        dve.tensor_reduce(mx_units[:, u % 2, :, u // 2],
                                          s_bank[u % 2][:].rearrange("p (h k) -> p h k", k=P),
                                          AX.X, ALU.max).then_inc(dve_max, 1)
                    if u == 0 and has(s - 2):
                        b = s - 2
                        xb = x1[:, bass.ds(b * D, D)]
                        dve.wait_ge(pe_out, count(b, 1))
                        dve.wait_ge(pool_xb, count(b, 1))
                        dve.tensor_tensor(xb, m1[:, 0:D], xb, ALU.add).then_inc(dve_x1, 1)
                        dve.wait_ge(dve_x1, count(b, 1))
                        dve.tensor_scalar(x1b[:], xb, 1.0, None, ALU.mult).then_inc(dve_bn, 1)
                        dve.wait_ge(dve_bn, count(b, 2, 1))
                        dve.bn_stats(bn2[:], x1b[:]).then_inc(dve_bn, 1)
                        dve.wait_ge(dve_bn, count(b, 2))
                        dve.tensor_tensor(st2[:, 0:2], bn2[:, 1:3], bn2[:, 4:6], ALU.add)
                        dve.tensor_tensor(st2[:, 2:3], bn2[:, 1:2], bn2[:, 4:5], ALU.subtract).then_inc(dve_stats, 1)
                        dve.wait_ge(dve_stats, count(b, 3, 1))
                        dve.tensor_scalar(mv2[:, 0:1], st2[:, 0:1], 0.5, None, ALU.mult)
                        dve.scalar_tensor_tensor(st2[:, 3:4], st2[:, 2:3], 0.25, st2[:, 2:3], ALU.mult, ALU.mult).then_inc(dve_stats, 1)
                        dve.wait_ge(dve_stats, count(b, 3, 2))
                        dve.scalar_tensor_tensor(mv2[:, 1:2], st2[:, 1:2], 1.0 / D, st2[:, 3:4], ALU.mult, ALU.add).then_inc(dve_stats, 1)
                    if u == 1 and has(s - 2):
                        b = s - 2
                        dve.wait_ge(dve_stats, count(b, 3))
                        rsqrt(dve, mv2[:, 1:2], rs2[:], nt2, nt2i[:], dve_chain, b * (RSQRT_OPS + 1))
                        dve.tensor_scalar(nt2[:, 0], rs2[:], XS, None, ALU.mult).then_inc(dve_chain, 1)
                        dve.wait_ge(dve_chain, count(b, RSQRT_OPS + 1))
                        if not peeled(b) or b >= 1:
                            dve.wait_ge(pe_x2T, count(b - 1, 1))
                            dve.wait_ge(pool_x2lo, count(b - 1, 1))
                        dve.tensor_scalar(x2f[:], x1b[:], mv2[:, 0:1], nt2[:, 0],
                                          ALU.subtract, ALU.mult).then_inc(dve_x2, 1)
                    if u == 2 and has(s + 2):
                        dve.wait_ge(pe_xT, count(s + 1, 1))
                        normalize(s + 2)
                if has(s):
                    dve.wait_ge(dve_max, count(s, UNITS))
                    dve.tensor_scalar(qx[par][:, :, MROW], mx[:], -1.0 / QS, None, ALU.mult).then_inc(dve_m, 1)
                if has(s - 2):
                    b = s - 2
                    dve.wait_ge(pe_gate, count(b, 1))
                    dve.tensor_tensor(logits[:, bass.ds(b, 1), :].rearrange("p a e -> p (a e)"), m1[:, 0:E], gb_bc[:], ALU.add).then_inc(dve_gate, 1)
                if has(s + 1):
                    if has(s - 1):
                        dve.wait_ge(pe_st, count(s - 1, UNITS))
                    evacuate(qT[1 - par], m0_16, pe_tq1, dve_tq1, s + 1)
                    evacuate(kT[1 - par], m1_16, pe_tk, dve_tk, s + 1)
                if has(s - 1):
                    b = s - 1
                    dve.wait_ge(pe_av, count(b, UNITS))
                    dve.reciprocal(recip[:], av_bank[:, :, HD]).then_inc(dve_rec, 1)
                    dve.wait_ge(dve_rec, count(b, 1))
                    if not peeled(b) or b >= 1:
                        dve.wait_ge(pe_attnT, count(b - 1, 1))
                    dve.tensor_tensor(attn[:].rearrange("p (h d) -> p h d", d=HD), av_bank[:, :, 0:HD],
                                      recip[:].rearrange("p (h a) -> p h a", a=1).to_broadcast([P, H, HD]),
                                      ALU.mult).then_inc(dve_norm, 1)
                if has(s):
                    evacuate(qT[par], m1_16, pe_tq2, dve_tq2, s)

            normalize(0)
            run_steps(dve, step)

        @block.tensor
        def _(pe):
            pe.wait_ge(consts_ready, 1)
            pe.wait_ge(small_loaded, 16 * 6)

            def pack_T(dst, src, done):
                for g in range(HG):
                    last = pe.transpose(dst[:, g * P:(g + 1) * P],
                                        src[:, g * ROWT:(g + 1) * ROWT, :].rearrange("p h d -> p (h d)"), ident16[:])
                last.then_inc(done, 1)

            def av(b, par, u):
                pe.wait_ge(act_exp, count(b, UNITS, u + 1))
                if u == 0:
                    pe.wait_ge(act_v, count(b, 1))
                    if not peeled(b) or b >= 1:
                        pe.wait_ge(dve_norm, count(b - 1, 1))
                for i in range(UH):
                    h = ((u % 2) * UH + i) * ROWT + u // 2
                    last = pe.matmul(av_bank[:, h, 0:VW], probs[u % NPB][:, i * P:(i + 1) * P], v[par][:, h, :],
                                     start=True, stop=True)
                last.then_inc(pe_av, 1)

            def scores(out_bank, stat, mov, rows, u, done):
                j = u // 2
                for i in range(UH):
                    g = (u % 2) * UH + i
                    last = pe.matmul(out_bank[:, i * P:(i + 1) * P], stat[SLOT * j:SLOT * j + rows, g, :],
                                     mov[SLOT * j:SLOT * j + rows, g, :], start=True, stop=True)
                last.then_inc(done, 1)

            def step(s, par):
                for u in range(UNITS):
                    if has(s):
                        if u == 0:
                            pe.wait_ge(dve_tq1, count(s, 1))
                            pe.wait_ge(dve_tk, count(s, 1))
                        if not peeled(s) or s * UNITS + u >= 2:
                            pe.wait_ge(dve_max, count(s, UNITS, u - 1))
                        scores(s_bank[u % 2], qT[par], kT[par], MROW, u, pe_s)
                    if has(s - 1):
                        b = s - 1
                        if u == 0:
                            pe.wait_ge(dve_tq2, count(b, 1))
                        if not peeled(b) or b * UNITS + u >= 2:
                            pe.wait_ge(act_exp, count(b, UNITS, u - 1))
                        scores(t_bank[u % 2], kT[1 - par], qT[1 - par], SLOT, u, pe_st)
                        if u >= 1:
                            av(b, 1 - par, u - 1)
                    if u == 0 and has(s - 2):
                        b = s - 2
                        pe.wait_ge(act_attnT, count(b, 1))
                        if has(b + 1):
                            pe.wait_ge(dve_tq2, count(b + 1, 1))
                        else:
                            pe.wait_ge(dve_gate, count(b - 1, 1))
                        for c in range(DC):
                            last = pe.matmul(m1[:, 0:D], attnT[:, c, :], wout_sb[:, c, :], start=(c == 0), stop=(c == DC - 1))
                        last.then_inc(pe_out, 1)
                    if u == 0 and has(s + 1):
                        b = s + 1
                        pe.wait_ge(dve_xhat, count(b, 1))
                        pe.wait_ge(ctx_loaded[1 - par], paired(b, 1 - par))
                        for c in range(DC):
                            pe.transpose(m0[:, c * P:(c + 1) * P], xhat[:, c * P:(c + 1) * P], ident[:])
                        pe.transpose(m0[:, DC * P:(DC + 1) * P], ctx_sb[:, 1 - par, :], ident[:]).then_inc(pe_xT, 1)
                    if u == 2 and has(s + 1):
                        b = s + 1
                        pe.wait_ge(act_xT, count(b, 1))
                        if has(s - 2):
                            pe.wait_ge(dve_x1, count(s - 2, 1))
                        for c in range(DC):
                            last = pe.matmul(m1[:, 0:D], xT[:, c, :], wq_sb[:, c, :], start=(c == 0), stop=(c == DC - 1))
                        last.then_inc(pe_q, 1)
                        pe.matmul(m2[:], xT[:, DC, :], wkv_sb[:], start=True, stop=True).then_inc(pe_kv, 1)
                    if u == 5 and has(s - 2):
                        b = s - 2
                        pe.wait_ge(dve_x2, count(b, 1))
                        for c in range(DC):
                            last = pe.transpose(m0[:, c * P:(c + 1) * P], x2f[:, c * P:(c + 1) * P], ident[:])
                        last.then_inc(pe_x2T, 1)
                    if u == 7 and has(s - 2):
                        b = s - 2
                        pe.wait_ge(act_x2T, count(b, 1))
                        if has(s + 1):
                            pe.wait_ge(act_qk, count(s + 1, 1))
                        for c in range(DC):
                            last = pe.matmul(m1[:, 0:E], x2T[:, c, :], gw_sb[:, c, :], start=(c == 0), stop=(c == DC - 1))
                        last.then_inc(pe_gate, 1)
                if has(s - 1):
                    av(s - 1, 1 - par, UNITS - 1)
                if has(s + 1):
                    b = s + 1
                    pe.wait_ge(pool_lo, count(b, 1))
                    if has(s - 2):
                        pe.wait_ge(act_x2T, count(s - 2, 1))
                    pack_T(m0_16, qx[1 - par], pe_tq1)
                    pe.wait_ge(act_qk, count(b, 1))
                    if has(s - 2):
                        pe.wait_ge(dve_gate, count(s - 2, 1))
                    pack_T(m1_16, kx, pe_tk)
                if has(s - 1):
                    b = s - 1
                    pe.wait_ge(dve_norm, count(b, 1))
                    if has(s + 1):
                        pe.wait_ge(act_v, count(s + 1, 1))
                    for c in range(DC):
                        last = pe.transpose(m2[:, c * P:(c + 1) * P], attn[:, c * P:(c + 1) * P], ident[:])
                    last.then_inc(pe_attnT, 1)
                if has(s):
                    pe.wait_ge(dve_m, count(s, 1))
                    if has(s + 1):
                        pe.wait_ge(dve_tk, count(s + 1, 1))
                    elif has(s - 2):
                        pe.wait_ge(dve_gate, count(s - 2, 1))
                    pack_T(m1_16, qx[par], pe_tq2)

            run_steps(pe, step)


def experts(nc, b1, b2, out, x1, logits, w1h, w1l, w2h, w2l, ident, ident16, x2_dram, ids_dram, y_dram):
    with ExitStack() as ctx:
        def sb(name, shape, dt):
            return ctx.enter_context(nc.sbuf_tensor(name, shape, dt))

        def bank(name, shape, dt):
            return ctx.enter_context(nc.psum_tensor(name, shape, dt))

        def sem(name):
            return ctx.enter_context(nc.semaphore(name))

        KT = 16
        below = sb("below", [P, P], F32)
        ones = sb("ones", [P, P], F32)
        iota_i = sb("iota_i", [P, 64], I32)
        iota_f = sb("iota_f", [P, 64], F32)
        token_ids = sb("token_ids", [P, B], I32)
        b1_rows = sb("b1_rows", [E * FC, P], F32)
        b1T = sb("b1T", [P, E * FC], F32)
        b2_bc = sb("b2_bc", [P, E * D], F32)
        prob = sb("prob", [P, B, E], F32)
        prob2 = sb("prob2", [P, B, E], F32)
        cand = sb("cand", [P, B, E], F32)
        first = sb("first", [P, B, E], F32)
        second = sb("second", [P, B, E], F32)
        chosen = sb("chosen", [P, B, E], F32)
        run = [sb(f"run{i}", [P, B, E], F32) for i in range(2)]
        slot_of = sb("slot_of", [P, B, E], F32)
        top = sb("top", [P, B], F32)
        top1 = sb("top1", [P, B], F32)
        top2 = sb("top2", [P, B], F32)
        norm = sb("norm", [P, B], F32)
        weight = [sb(f"weight{i}", [P, B], F32) for i in range(2)]
        slot_f = sb("slot_f", [P, 2, B], F32)
        slot_i = sb("slot_i", [P, 2, B], I32)
        over = sb("over", [P, E, KT], F32)
        tiles = [sb(f"tiles{i}", [P, E], F32) for i in range(3)]
        past = sb("past", [1, TILES + 1, E], F32)
        tile_f = sb("tile_f", [1, TILES + 1], F32)
        tile_expert = sb("tile_expert", [1, TILES + 1], I32)
        ids_rows = sb("ids_rows", [TILES, P], I32)
        ids_f = sb("ids_f", [TILES, P], F32)
        ids = sb("ids", [P, TILES], I32)
        spare = sb("spare", [P, 1], F32)
        tile_ids = [sb(f"tile_ids{i}", [P, 1], I32) for i in range(2)]
        xg = [sb(f"xg{i}", [P, 2 * D], F16) for i in range(2)]
        xgT = [sb(f"xgT{i}", [P, 2 * DC, P], F16) for i in range(2)]
        h = [sb(f"h{i}", [P, FC * P], F32) for i in range(2)]
        hh = [sb(f"hh{i}", [P, FC * P], F16) for i in range(2)]
        hl = [sb(f"hl{i}", [P, FC * P], F16) for i in range(2)]
        y = [sb(f"y{i}", [P, D], F32) for i in range(2)]
        NG = 4
        ya = [sb(f"ya{i}", [P, D], F32) for i in range(NG)]
        yb = [sb(f"yb{i}", [P, D], F32) for i in range(NG)]

        h_bank = [bank(f"h_bank{i}", [P, 512], F32) for i in range(4)]
        x_bank = bank("x_bank", [P, 1024], F16)
        y_bank = [bank(f"y_bank{i}", [P, 512], F32) for i in range(2)]
        r_bank = bank("r_bank", [P, 512], F32)

        names = """consts1 consts2 loaded shifted exp_ready routed ranks_ready slots_ready b1_ready
        scattered ids_loaded ids_ready idsT_ready ids_int pe_b1 table_ready pool_ids
        pe_x pe_h pe_y dve_x dve_hi dve_lo dve_y act_h combined stored""".split()
        sems = {n: sem("e_" + n) for n in names}
        (consts1, consts2, loaded, shifted, exp_ready, routed, ranks_ready, slots_ready, b1_ready,
         scattered, ids_loaded, ids_ready, idsT_ready, ids_int, pe_b1, table_ready, pool_ids,
         pe_x, pe_h, pe_y, dve_x, dve_hi, dve_lo, dve_y, act_h, combined, stored) = [sems[n] for n in names]
        x_gathered = [sem(f"x_gathered{i}") for i in range(2)]
        y_stored = [sem(f"y_stored{i}") for i in range(2)]
        y_gathered = [sem(f"y_gathered{i}") for i in range(NG)]

        def shared(i, par, lots=16):
            return lots // 2 * i + (lots if par == 0 else lots // 2)

        def later(i, n=1):
            return not isinstance(i, int) or i >= n

        def run_tiles(eng, step):
            for i in range(-1, 2):
                step(i, i % 2)
            with eng.Fori(1, (TILES - 1) // 2) as pair:
                step(2 * pair, 0)
                step(2 * pair + 1, 1)
            step(TILES - 1, 0)

        def bc(ap, shape, at):
            s = {1: "p (a n) -> p a n", 2: "p (n a) -> p n a"}[at]
            return ap.rearrange(s, a=1).to_broadcast(shape)

        block = ctx.enter_context(nc.Block())

        @block.sync
        def _(sp):
            sp.dma_start(b1_rows[:], b1.rearrange("e (c p) -> (e c) p", p=P)).then_inc(loaded, 16)
            sp.dma_start(b2_bc[:], b2.rearrange("(a e) d -> a (e d)", a=1).to_broadcast([P, E * D])).then_inc(loaded, 16)
            sp.wait_ge(scattered, 16 * 2 * B)
            sp.dma_start(ids_rows[:], ids_dram.rearrange("(t p) a -> t (p a)", p=P)).then_inc(ids_loaded, 16)

            def step(i, par):
                if not isinstance(i, int) or i >= 0:
                    sp.wait_ge(dve_y, count(i, 1))
                    sp.dma_start(y_dram[bass.ds(i * P, P), :], y[par][:]).then_inc(y_stored[par], 16)

            run_tiles(sp, step)
            for b in range(B):
                sp.wait_ge(combined, b + 1)
                sp.dma_start(out[b], x1[:, b * D:(b + 1) * D]).then_inc(stored, 16)
            sp.wait_ge(stored, 16 * B)

        @block.gpsimd
        def _(pool):
            pool.memset(ones[:], 1.0).then_inc(consts1, 1)
            pool.iota(iota_i[:], pattern=[[1, 64]], base=0, channel_multiplier=0).then_inc(consts1, 1)
            pool.iota(token_ids[:], pattern=[[P, B]], base=0, channel_multiplier=1).then_inc(consts1, 1)
            pool.wait_ge(consts1, 3)
            pool.affine_select(out=below[:], in_=ones[:], compare_op=ALU.is_gt, fill=0.0, base=0,
                               pattern=[[1, P]], channel_multiplier=-1).then_inc(consts1, 1)
            pool.tensor_copy(iota_f[:], iota_i[:]).then_inc(consts1, 1)
            pool.wait_ge(slots_ready, 1)
            for b in range(B):
                for k in range(2):
                    pool.indirect_dma_start(out=ids_dram, out_offset=bass.IndirectOffsetOnAxis(ap=slot_i[:, k, b:b + 1], axis=0),
                                            in_=token_ids[:, b:b + 1], in_offset=None).then_inc(scattered, 16)

            def gather_x(i, par):
                pool.wait_ge(consts1, 5)
                pool.tensor_copy(tile_ids[par][:], ids[:, bass.ds(i, 1)]).then_inc(pool_ids, 1)
                pool.wait_ge(pool_ids, count(i, 1))
                if not isinstance(i, int):
                    pool.tensor_tensor(spare[:], ones[:, 0:1], ones[:, 0:1], ALU.mult)
                pool.indirect_dma_start(out=xg[par][:], out_offset=None, in_=x2_dram,
                                        in_offset=bass.IndirectOffsetOnAxis(ap=tile_ids[par][:], axis=0)).then_inc(x_gathered[par], 16)

            pool.wait_ge(ids_int, 1)

            def step(i, par):
                if isinstance(i, int) and i + 1 >= TILES:
                    return
                if later(i, 1):
                    pool.wait_ge(pe_x, count(i - 1, 1))
                gather_x(i + 1, 1 - par)

            run_tiles(pool, step)
            for i in range(2):
                pool.wait_ge(y_stored[i], 16 * ((TILES + 1 - i) // 2))
            for b in range(B):
                if b >= NG:
                    pool.wait_ge(combined, b - NG + 1)
                for k, rows in ((0, ya), (1, yb)):
                    pool.indirect_dma_start(out=rows[b % NG][:], out_offset=None, in_=y_dram,
                                            in_offset=bass.IndirectOffsetOnAxis(ap=slot_i[:, k, b:b + 1], axis=0)
                                            ).then_inc(y_gathered[b % NG], 16)

        @block.scalar
        def _(act):
            act.wait_ge(shifted, 1)
            act.activation(prob[:], prob[:], ACT.Exp).then_inc(exp_ready, 1)
            act.wait_ge(table_ready, 1)
            act.wait_ge(b1_ready, 1)

            def step(i, par):
                if isinstance(i, int) and i + 1 >= TILES:
                    return
                t = i + 1
                e = nc.values_load(tile_expert[0:1, bass.ds(t, 1)], engines=[mybir.EngineType.Activation],
                                   min_val=0, max_val=E - 1)
                for k in range(2):
                    act.wait_ge(pe_h, count(t, 2, k + 1))
                    if k == 0 and later(t, 2):
                        act.wait_ge(dve_lo, count(t - 2, 2))
                    for c in range(4):
                        f = 4 * k + c
                        last = act.activation(h[1 - par][:, f * P:(f + 1) * P], h_bank[2 * (1 - par) + k][:, c * P:(c + 1) * P],
                                              ACT.Gelu_apprx_tanh, bias=b1T[:, bass.ds(e * FC + f, 1)], scale=1.0 / (XS * WS))
                    last.then_inc(act_h, 1)

            run_tiles(act, step)

        @block.vector
        def _(dve):
            n = [0]

            def chain(ins):
                n[0] += 1
                ins.then_inc(routed, 1)
                dve.wait_ge(routed, n[0])

            full = [P, B, E]
            chain(dve.tensor_reduce(top[:], logits[:], AX.X, ALU.max))
            dve.tensor_tensor(prob[:], logits[:], bc(top[:], full, 2), ALU.subtract).then_inc(shifted, 1)
            dve.wait_ge(exp_ready, 1)
            chain(dve.tensor_reduce(norm[:], prob[:], AX.X, ALU.add))
            chain(dve.reciprocal(norm[:], norm[:]))
            chain(dve.tensor_tensor(prob[:], prob[:], bc(norm[:], full, 2), ALU.mult))
            dve.wait_ge(consts1, 5)
            experts_iota = iota_f[:, 0:E].rearrange("p (a e) -> p a e", a=1).to_broadcast(full)

            def best(p, value, mask):
                chain(dve.tensor_reduce(value[:], p[:], AX.X, ALU.max))
                chain(dve.tensor_tensor(cand[:], p[:], bc(value[:], full, 2), ALU.is_equal))
                chain(dve.scalar_tensor_tensor(cand[:], cand[:], -float(E), experts_iota, ALU.mult, ALU.add))
                chain(dve.tensor_reduce(norm[:], cand[:], AX.X, ALU.min))
                chain(dve.tensor_tensor(mask[:], cand[:], bc(norm[:], full, 2), ALU.is_equal))

            best(prob, top1, first)
            chain(dve.scalar_tensor_tensor(prob2[:], first[:], -2.0, prob[:], ALU.mult, ALU.add))
            best(prob2, top2, second)
            dve.tensor_tensor(chosen[:], first[:], second[:], ALU.add).then_inc(consts2, 1)
            chain(dve.tensor_tensor(norm[:], top1[:], top2[:], ALU.add))
            chain(dve.reciprocal(norm[:], norm[:]))
            chain(dve.tensor_tensor(weight[0][:], top1[:], norm[:], ALU.mult))
            chain(dve.tensor_tensor(weight[1][:], top2[:], norm[:], ALU.mult))
            dve.wait_ge(ranks_ready, 1)
            ranks = r_bank[:, 0:P].rearrange("p (b e) -> p b e", e=E)
            totals = r_bank[:, P:2 * P].rearrange("p (b e) -> p b e", e=E)
            chain(dve.memset(run[0][:, 0:1, :], 0.0))
            chain(dve.tensor_copy(run[0][:, 1:B, :], totals[:, 0:B - 1, :]))
            src = 0
            for d in (1, 2, 4, 8):
                a, z = run[src], run[1 - src]
                chain(dve.tensor_copy(z[:, 0:d, :], a[:, 0:d, :]))
                chain(dve.tensor_tensor(z[:, d:B, :], a[:, d:B, :], a[:, 0:B - d, :], ALU.add))
                src = 1 - src
            before = run[src]
            chain(dve.tensor_tensor(top[:, 0:E], totals[:, B - 1, :], before[:, B - 1, :], ALU.add))
            thresholds = iota_f[:, 0:KT].rearrange("p (a k) -> p a k", a=1).to_broadcast([P, E, KT])
            chain(dve.tensor_scalar(tiles[2][:], top[:, 0:E], 1.0 / P, None, ALU.mult))
            chain(dve.tensor_tensor(over[:], bc(tiles[2][:], [P, E, KT], 2), thresholds, ALU.is_gt))
            chain(dve.tensor_reduce(tiles[0][:], over[:], AX.X, ALU.add))
            chain(dve.tensor_copy(tiles[2][:], tiles[0][:]))
            src = 0
            for d in (1, 2, 4):
                a, z = tiles[src], tiles[1 - src]
                chain(dve.tensor_copy(z[:, 0:d], a[:, 0:d]))
                chain(dve.tensor_tensor(z[:, d:E], a[:, d:E], a[:, 0:E - d], ALU.add))
                src = 1 - src
            ends = tiles[src]
            chain(dve.tensor_tensor(past[:], ends[0:1, :].rearrange("p (a e) -> p a e", a=1).to_broadcast([1, TILES + 1, E]),
                                    iota_f[0:1, 0:TILES + 1].rearrange("p (t a) -> p t a", a=1).to_broadcast([1, TILES + 1, E]), ALU.is_le))
            chain(dve.tensor_reduce(tile_f[:], past[:], AX.X, ALU.add))
            dve.tensor_scalar(tile_expert[:], tile_f[:], float(E - 1), None, ALU.min).then_inc(table_ready, 1)
            chain(dve.tensor_tensor(tiles[2][:], ends[:], tiles[2][:], ALU.subtract))
            chain(dve.tensor_tensor(slot_of[:], before[:], ranks, ALU.add))
            chain(dve.scalar_tensor_tensor(slot_of[:], bc(tiles[2][:], full, 1), float(P), slot_of[:], ALU.mult, ALU.add))
            for k, mask in enumerate((first, second)):
                chain(dve.tensor_tensor(cand[:], mask[:], slot_of[:], ALU.mult))
                chain(dve.tensor_reduce(slot_f[:, k, :], cand[:], AX.X, ALU.add))
            dve.tensor_copy(slot_i[:], slot_f[:]).then_inc(slots_ready, 1)
            dve.wait_ge(pe_b1, 1)
            dve.tensor_copy(b1T[:], h_bank[0][:, 0:E * FC]).then_inc(b1_ready, 1)
            dve.wait_ge(ids_loaded, 16)
            dve.tensor_copy(ids_f[:], ids_rows[:]).then_inc(ids_ready, 1)
            dve.wait_ge(idsT_ready, 1)
            dve.tensor_copy(ids[:], r_bank[:, 0:TILES]).then_inc(ids_int, 1)
            dve.wait_ge(loaded, 32)

            def step(i, par):
                nxt = not isinstance(i, int) or i + 1 < TILES
                cur = not isinstance(i, int) or i >= 0
                if nxt:
                    t = i + 1
                    dve.wait_ge(pe_x, count(t, 1))
                    if later(t, 2):
                        dve.wait_ge(pe_h, count(t - 2, 2))
                    dve.tensor_copy(xgT[1 - par][:], x_bank[:, 0:2 * D].rearrange("p (c t) -> p c t", t=P)).then_inc(dve_x, 1)
                if cur:
                    e = nc.values_load(tile_expert[0:1, bass.ds(i, 1)], engines=[mybir.EngineType.DVE],
                                       min_val=0, max_val=E - 1)
                    dve.wait_ge(pe_y, count(i, 1))
                    if later(i, 2):
                        dve.wait_ge(y_stored[par], shared(i - 2, par))
                    dve.scalar_tensor_tensor(y[par][:], y_bank[par][:, 0:D], 1.0 / (XS * WS), b2_bc[:, bass.ds(e * D, D)],
                                             ALU.mult, ALU.add).then_inc(dve_y, 1)
                if nxt:
                    t = i + 1
                    for k in range(2):
                        half = slice(k * 512, (k + 1) * 512)
                        dve.wait_ge(act_h, count(t, 2, k + 1))
                        if k == 0 and later(t, 2):
                            dve.wait_ge(pe_y, count(t - 2, 1))
                        dve.tensor_scalar(hh[1 - par][:, half], h[1 - par][:, half], XS, None, ALU.mult).then_inc(dve_hi, 1)
                        dve.wait_ge(dve_hi, count(t, 2, k + 1))
                        dve.scalar_tensor_tensor(hl[1 - par][:, half], h[1 - par][:, half], XS, hh[1 - par][:, half],
                                                 ALU.mult, ALU.subtract).then_inc(dve_lo, 1)

            run_tiles(dve, step)
            for b in range(B):
                xb = x1[:, b * D:(b + 1) * D]
                dve.wait_ge(y_gathered[b % NG], 32 * (b // NG + 1))
                chain(dve.scalar_tensor_tensor(xb, ya[b % NG][:], weight[0][:, b:b + 1], xb, ALU.mult, ALU.add))
                dve.scalar_tensor_tensor(xb, yb[b % NG][:], weight[1][:, b:b + 1], xb, ALU.mult, ALU.add).then_inc(combined, 1)

        @block.tensor
        def _(pe):
            pe.wait_ge(consts1, 5)
            pe.wait_ge(consts2, 1)
            flat = chosen[:].rearrange("p b e -> p (b e)")
            pe.matmul(r_bank[:, 0:P], below[:], flat, start=True, stop=True)
            pe.matmul(r_bank[:, P:2 * P], ones[:], flat, start=True, stop=True).then_inc(ranks_ready, 1)
            pe.wait_ge(loaded, 32)
            pe.transpose(h_bank[0][:, 0:E * FC], b1_rows[:], ident[0:E * FC, 0:E * FC]).then_inc(pe_b1, 1)
            pe.wait_ge(ids_ready, 1)
            pe.transpose(r_bank[:, 0:TILES], ids_f[:], ident[0:TILES, 0:TILES]).then_inc(idsT_ready, 1)
            pe.wait_ge(b1_ready, 1)
            pe.wait_ge(table_ready, 1)

            def step(i, par):
                nxt = not isinstance(i, int) or i + 1 < TILES
                cur = not isinstance(i, int) or i >= 0
                if nxt:
                    t = i + 1
                    tp = 1 - par
                    e = nc.values_load(tile_expert[0:1, bass.ds(t, 1)], engines=[mybir.EngineType.PE],
                                       min_val=0, max_val=E - 1)
                    pe.wait_ge(x_gathered[tp], shared(t, tp))
                    if later(t, 1):
                        pe.wait_ge(dve_x, count(t - 1, 1))
                    for c in range(2 * DC):
                        last = pe.transpose(x_bank[:, c * P:(c + 1) * P], xg[tp][:, c * P:(c + 1) * P], ident16[:])
                    last.then_inc(pe_x, 1)
                    pe.wait_ge(dve_x, count(t, 1))
                    for k in range(2):
                        if later(t, 2):
                            pe.wait_ge(act_h, count(t - 2, 2, k + 1))
                        for c in range(4):
                            f = 4 * k + c
                            terms = [(w, x, d) for d in range(DC) for w, x in ((w1h, 0), (w1h, DC), (w1l, 0))]
                            for m, (w, x, d) in enumerate(terms):
                                last = pe.matmul(h_bank[2 * tp + k][:, c * P:(c + 1) * P],
                                                 w[:, bass.ds(e * (DC * F) + (d * F + f * P), P)], xgT[tp][:, x + d, :],
                                                 start=(m == 0), stop=(m == len(terms) - 1))
                        last.then_inc(pe_h, 1)
                if cur:
                    e = nc.values_load(tile_expert[0:1, bass.ds(i, 1)], engines=[mybir.EngineType.PE],
                                       min_val=0, max_val=E - 1)
                    if later(i, 2):
                        pe.wait_ge(dve_y, count(i - 2, 1))
                    for f in range(FC):
                        if f % 4 == 0:
                            pe.wait_ge(dve_lo, count(i, 2, f // 4 + 1))
                        for m, (a, w) in enumerate(((hh, w2h), (hl, w2h), (hh, w2l))):
                            last = pe.matmul(y_bank[par][:, 0:D], a[par][:, f * P:(f + 1) * P],
                                             w[:, bass.ds(e * (FC * D) + f * D, D)],
                                             start=(f == 0 and m == 0), stop=(f == FC - 1 and m == 2))
                    last.then_inc(pe_y, 1)

            run_tiles(pe, step)


_INS = ['x', 'ctx_1024', 'fside_BxSx2_0', 'L0_xattn_Wq', 'L0_xattn_Wkv', 'L0_xattn_Wout', 'L0_xattn_bout',
        'L0_ffn_gate_w', 'L0_ffn_gate_b', 'L0_ffn_w1', 'L0_ffn_b1', 'L0_ffn_w2', 'L0_ffn_b2']
_OUTS = [((16, 128, 256), 'float32')]


def kernel(**inputs):
    import numpy as _np
    import concourse.bacc as _bacc
    from concourse import mybir as _mybir
    from concourse.bass_utils import run_bass_kernel_spmd as _run

    nc = _bacc.Bacc("TRN2", target_bir_lowering=False, num_devices=1)
    arrays, args = {}, []
    for name in _INS:
        a = _np.ascontiguousarray(inputs[name])
        arrays[f"in_{name}_dram"] = a
        args.append(nc.dram_tensor(f"in_{name}_dram", a.shape, _mybir.dt.from_np(a.dtype), kind="ExternalInput").ap())
    for i, (shape, dtype) in enumerate(_OUTS):
        dt = _mybir.dt.from_np(_np.dtype(dtype))
        args.append(nc.dram_tensor(f"out_{i}_dram", shape, dt, kind="ExternalOutput").ap())
    build(nc, *args)
    r = _run(nc, [arrays], core_ids=[0])
    got = tuple(r.results[0][f"out_{i}_dram"] for i in range(len(_OUTS)))
    return got[0]
```

```python
from contextlib import ExitStack
import math

import numpy as np
import concourse.bass as bass
from concourse import mybir

F32 = mybir.dt.float32
F16 = mybir.dt.float16
I32 = mybir.dt.int32
ALU = mybir.AluOpType
ACT = mybir.ActivationFunctionType
AX = mybir.AxisListType

P = 128
B = 16
D = 256
DC = D // P
CD = 128
H = 32
HD = D // H
SLOT = 32
ROWT = P // SLOT
HG = H // ROWT
UNITS = 8
UH = H // UNITS
VW = SLOT
HALF = UNITS // 2
FIRST = 4
NPB = 2
E = 8
F = 1024
FC = F // P
EPS = 1e-5
QS = 64.0
XS = 64.0
WS = 256.0
MROW = 3 * HD
EXP_SCALE = 1.0 / (QS * QS * math.sqrt(HD))
TWO_PI = 2.0 * math.pi
TILES = 2 * B + E - 1
RSQRT_OPS = 15
CHAIN2 = 11
RSQRT_MAGIC = float(0x5F3759DF)


def count(b, per, k=None):
    return b * per + (per if k is None else k)


def rsqrt(eng, var, y, t, ti, done, base):
    n = [0]

    def chain(ins):
        n[0] += 1
        ins.then_inc(done, 1)
        eng.wait_ge(done, base + n[0])

    chain(eng.tensor_scalar(t[:, 0], var, EPS, None, ALU.add))
    chain(eng.tensor_copy(t[:, 1], t[:, 0].bitcast(I32)))
    chain(eng.tensor_scalar(ti, t[:, 1], -0.5, RSQRT_MAGIC, ALU.mult, ALU.add))
    guess = ti.bitcast(F32)
    for i in range(3):
        y_in = guess if i == 0 else y
        chain(eng.tensor_tensor(t[:, 1], y_in, y_in, ALU.mult))
        chain(eng.tensor_tensor(t[:, 2], t[:, 1], t[:, 0], ALU.mult))
        chain(eng.tensor_scalar(t[:, 2], t[:, 2], -0.5, 1.5, ALU.mult, ALU.add))
        chain(eng.tensor_tensor(y, y_in, t[:, 2], ALU.mult))


def build(nc, x, ctx_in, pos, wq, wkv, wout, bout, gate_w, gate_b, w1, b1, w2, b2, out):
    with ExitStack() as ctx:
        def sb(name, shape, dt):
            return ctx.enter_context(nc.sbuf_tensor(name, shape, dt))

        x1 = sb("x1", [P, B * D], F32)
        logits = sb("logits", [P, B, E], F32)
        w1h = sb("w1h", [P, E * DC * F], F16)
        w1l = sb("w1l", [P, E * DC * F], F16)
        w2h = sb("w2h", [P, E * FC * D], F16)
        w2l = sb("w2l", [P, E * FC * D], F16)
        ident = sb("ident", [P, P], F32)
        ident16 = sb("ident16", [P, P], F16)

        x2_dram = nc.dram_tensor("x2_dram", (B * P, 2 * D), F16, kind="Internal").ap()
        y_dram = nc.dram_tensor("y_dram", (2 * B * P + TILES * P, D), F32, kind="Internal").ap()

        attention(nc, x, ctx_in, pos, wq, wkv, wout, bout, gate_w, gate_b, w1, w2,
                  x1, logits, w1h, w1l, w2h, w2l, ident, ident16, x2_dram)
        experts(nc, b1, b2, out, x1, logits, w1h, w1l, w2h, w2l, ident, ident16, x2_dram, y_dram)


def attention(nc, x, ctx_in, pos, wq, wkv, wout, bout, gate_w, gate_b, w1, w2,
              x1, logits, w1h, w1l, w2h, w2l, ident, ident16, x2_dram):
    w1_chunks = w1.rearrange("e (k p) f -> (e k) p f", p=P)
    w2_chunks = w2.rearrange("e (h c p) d -> (e h) p c d", p=P, h=2)

    with ExitStack() as ctx:
        def sb(name, shape, dt):
            return ctx.enter_context(nc.sbuf_tensor(name, shape, dt))

        def bank(name, shape, dt):
            return ctx.enter_context(nc.psum_tensor(name, shape, dt))

        def sem(name):
            return ctx.enter_context(nc.semaphore(name))

        wq_sb = sb("wq_sb", [P, DC, D], F32)
        wkv_sb = sb("wkv_sb", [P, 2 * D], F32)
        wout_sb = sb("wout_sb", [P, DC, D], F32)
        bout_bc = sb("bout_bc", [P, D], F32)
        gw_sb = sb("gw_sb", [P, DC, E], F32)
        gb_bc = sb("gb_bc", [P, E], F32)
        pos_sb = sb("pos_sb", [P, B, 2], F32)
        cos8 = sb("cos8", [P, B * HD], F32)
        sin8 = sb("sin8", [P, B * HD], F32)
        bn1 = sb("bn1", [P, B * 6], F32)
        mv1 = sb("mv1", [P, B * 2], F32)
        rs1 = sb("rs1", [P, B], F32)
        nt1 = sb("nt1", [P, 3, B], F32)
        nt1i = sb("nt1i", [P, B], I32)
        bn2 = sb("bn2", [P, 6], F32)
        mv2 = sb("mv2", [P, 2], F32)
        rs2 = sb("rs2", [P, 1], F32)
        nt2 = sb("nt2", [P, 3], F32)
        nt2i = sb("nt2i", [P, 1], I32)
        ctx_sb = sb("ctx_sb", [P, 2, CD], F32)
        xhat = sb("xhat", [P, D], F32)
        xT = sb("xT", [P, DC, P], F32)
        ctxT = [sb(f"ctxT{i}", [P, P], F32) for i in range(2)]
        qk = sb("qk", [P, 2, D], F32)
        qks = sb("qks", [P, 2, D], F32)
        qx = [sb(f"qx{i}", [P, H, SLOT], F16) for i in range(2)]
        kx = sb("kx", [P, H, SLOT], F16)
        qT = [sb(f"qT{i}", [P, HG, P], F16) for i in range(2)]
        kT = [sb(f"kT{i}", [P, HG, P], F16) for i in range(2)]
        v = [sb(f"v{i}", [P, H, VW], F32) for i in range(2)]
        mx = sb("mx", [P, H], F32)
        probs = [sb(f"probs{i}", [P, UH * P], F32) for i in range(NPB)]
        recip = sb("recip", [P, HALF * UH], F32)
        o_sb = [sb(f"o_sb{i}", [P, HALF * P], F32) for i in range(2)]
        attn = sb("attn", [P, D], F32)
        turned = sb("turned", [P, DC, P], F32)
        x1b = sb("x1b", [P, D], F32)
        x2f = sb("x2f", [P, D], F32)
        x2 = sb("x2", [P, 2, 2 * D], F16)
        w1_stage = sb("w1_stage", [P, F], F32)
        w2_stage = sb("w2_stage", [P, F], F32)
        ang, turns, turns_i, sincos = [o_sb[0][:, i * P:(i + 1) * P].rearrange("p (k n) -> p k n", k=2) for i in range(4)]
        turns_i = turns_i.bitcast(I32)

        s_bank = [bank(f"s_bank{i}", [P, 512], F32) for i in range(2)]
        t_bank = [bank(f"t_bank{i}", [P, 512], F32) for i in range(2)]
        o_bank = bank("o_bank", [P, HALF * P], F32)
        m0 = bank("m0", [P, 512], F32)
        m1 = bank("m1", [P, 512], F32)
        m2 = bank("m2", [P, 512], F32)
        tq1_16 = m0[:, :].bitcast(F16)
        tk_16 = s_bank[0][:, :].bitcast(F16)
        tq2_16 = s_bank[1][:, :].bitcast(F16)

        names = """consts_ready setup_v setup_a setup_p x_loaded x_rest_loaded pos_loaded small_loaded
        w1_loaded w2_loaded tables_ready slots_ready stats1_ready
        pe_xT pe_qk pe_v pe_tk pe_tq1 pe_tq2 pe_s pe_st pe_av pe_oT pe_attnT pe_out pe_x2T pe_gate
        act_xT act_qk act_v act_tk act_x1 act_hi act_exp act_o act_attnT act_x2hi act_x2T act_w
        dve_ws dve_max dve_m dve_tq1 dve_tq2 dve_rec dve_norm dve_x1 dve_bn dve_stats dve_gate
        dve_xhat pool_xb pool_mul pool_rope pool_lo dve_chain dve_x2 pool_x2lo pool_w""".split()
        sems = {n: sem(n) for n in names}
        (consts_ready, setup_v, setup_a, setup_p, x_loaded, x_rest_loaded, pos_loaded, small_loaded,
         w1_loaded, w2_loaded, tables_ready, slots_ready, stats1_ready,
         pe_xT, pe_qk, pe_v, pe_tk, pe_tq1, pe_tq2, pe_s, pe_st, pe_av, pe_oT, pe_attnT, pe_out, pe_x2T, pe_gate,
         act_xT, act_qk, act_v, act_tk, act_x1, act_hi, act_exp, act_o, act_attnT, act_x2hi, act_x2T, act_w,
         dve_ws, dve_max, dve_m, dve_tq1, dve_tq2, dve_rec, dve_norm, dve_x1, dve_bn, dve_stats, dve_gate,
         dve_xhat, pool_xb, pool_mul, pool_rope, pool_lo, dve_chain, dve_x2, pool_x2lo, pool_w) = [sems[n] for n in names]
        ctx_loaded = [sem(f"ctx_loaded{i}") for i in range(2)]
        x2_stored = [sem(f"x2_stored{i}") for i in range(2)]

        def paired(b, par):
            return 8 * b + (16 if par == 0 else 8)

        def run_steps(eng, step):
            for s in range(-2, 4):
                step(s, s % 2)
            with eng.Fori(2, B // 2 - 2) as pair:
                step(2 * pair, 0)
                step(2 * pair + 1, 1)
            for s in range(B - 4, B + 3):
                step(s, s % 2)

        def has(b):
            return not isinstance(b, int) or 0 <= b < B

        def peeled(s):
            return isinstance(s, int)

        block = ctx.enter_context(nc.Block())

        @block.sync
        def _(sp):
            sp.dma_start(pos_sb[:], pos.rearrange("b p c -> p b c")).then_inc(pos_loaded, 16)
            x1_by_batch = x1[:, :].rearrange("p (b d) -> p b d", b=B)
            x_by_batch = x.rearrange("b p d -> p b d")
            sp.dma_start(x1_by_batch[:, 0:FIRST], x_by_batch[:, 0:FIRST]).then_inc(x_loaded, 16)
            for i in range(2):
                sp.dma_start(ctx_sb[:, i, :], ctx_in[i]).then_inc(ctx_loaded[i], 16)
            sp.dma_start(wq_sb[:], wq.rearrange("(c p) n -> p c n", p=P)).then_inc(small_loaded, 16)
            sp.dma_start(wkv_sb[:], wkv).then_inc(small_loaded, 16)
            sp.dma_start(x1_by_batch[:, FIRST:B], x_by_batch[:, FIRST:B]).then_inc(x_rest_loaded, 16)
            wout_heads = wout.rearrange("(a i j d) n -> a j i d n", a=2, i=UH, d=HD)
            for u in range(UNITS):
                sp.dma_start(wout_sb[(u % HALF) * SLOT:(u % HALF + 1) * SLOT, u // HALF, :],
                             wout_heads[u % 2, u // 2]).then_inc(small_loaded, 16)
            sp.dma_start(gw_sb[:], gate_w.rearrange("(c p) n -> p c n", p=P)).then_inc(small_loaded, 16)
            sp.dma_start(bout_bc[:], bout.rearrange("(a d) -> a d", a=1).to_broadcast([P, D])).then_inc(small_loaded, 16)
            sp.dma_start(gb_bc[:], gate_b.rearrange("(a d) -> a d", a=1).to_broadcast([P, E])).then_inc(small_loaded, 16)

            def step(s, par):
                c = s + 4
                if has(c):
                    sp.wait_ge(pe_xT, count(s + 2, 1))
                    sp.dma_start(ctx_sb[:, par, :], ctx_in[c] if peeled(s) else ctx_in[bass.ds(c, 1)].rearrange("a p c -> (a p) c")).then_inc(ctx_loaded[par], 16)
                if has(s + 1):
                    if has(s):
                        sp.wait_ge(act_w, count(s, 2))
                        sp.wait_ge(pool_w, count(s, 2))
                    c = s + 1
                    one = w1_chunks[c] if peeled(s) else w1_chunks[bass.ds(c, 1)].rearrange("a p f -> (a p) f")
                    two = w2_chunks[c] if peeled(s) else w2_chunks[bass.ds(c, 1)].rearrange("a p c d -> (a p) c d")
                    sp.dma_start(w1_stage[:], one).then_inc(w1_loaded, 16)
                    sp.dma_start(w2_stage[:].rearrange("p (c d) -> p c d", d=D), two).then_inc(w2_loaded, 16)

                b = s - 2
                if has(b):
                    sp.wait_ge(pool_x2lo, count(b, 1))
                    sp.dma_start(x2_dram[bass.ds(b * P, P), :], x2[:, par, :]).then_inc(x2_stored[par], 16)

            run_steps(sp, step)
            for i in range(2):
                sp.wait_ge(x2_stored[i], 16 * (B // 2))

        @block.gpsimd
        def _(pool):
            pool.memset(ident[:], 0.0).then_inc(setup_p, 1)
            pool.wait_ge(setup_p, 1)
            pool.affine_select(out=ident[:], in_=ident[:], compare_op=ALU.not_equal, fill=1.0, base=0,
                               pattern=[[-1, P]], channel_multiplier=1).then_inc(setup_p, 1)
            pool.wait_ge(setup_p, 2)
            pool.tensor_copy(ident16[:], ident[:]).then_inc(consts_ready, 1)
            pool.memset(qx[0][:], 0.0)
            pool.memset(qx[1][:], 0.0)
            pool.memset(kx[:], 0.0).then_inc(setup_p, 1)
            pool.memset(v[0][:], 1.0)
            pool.memset(v[1][:], 1.0)
            pool.wait_ge(setup_p, 3)
            pool.memset(kx[:, :, MROW], QS).then_inc(slots_ready, 1)

            def alone():
                pool.wait_ge(consts_ready, 1)

            def add_bias(b):
                pool.wait_ge(dve_xhat, count(b, 1))
                alone()
                xb = x1[:, bass.ds(b * D, D)]
                pool.tensor_tensor(xb, xb, bout_bc[:], ALU.add).then_inc(pool_xb, 1)

            def step(s, par):
                b = s + 1
                if has(b):
                    pool.wait_ge(act_hi, count(b, 1))
                    q4 = qx[1 - par][:].rearrange("p h (k d) -> p h k d", d=HD)
                    k4 = kx[:].rearrange("p h (k d) -> p h k d", d=HD)
                    pool.tensor_tensor(q4[:, :, 2, :], qk[:, 0, :].rearrange("p (h d) -> p h d", d=HD), q4[:, :, 0, :],
                                       ALU.subtract)
                    pool.tensor_tensor(k4[:, :, 1, :], qk[:, 1, :].rearrange("p (h d) -> p h d", d=HD), k4[:, :, 0, :],
                                       ALU.subtract).then_inc(pool_lo, 1)
                if has(s):
                    pool.wait_ge(act_w, count(s, 2, 1))
                    alone()
                    pool.tensor_tensor(w1l[:, bass.ds(s * F, F)], w1_stage[:], w1h[:, bass.ds(s * F, F)],
                                       ALU.subtract).then_inc(pool_w, 1)
                    pool.wait_ge(act_w, count(s, 2))
                    alone()
                    pool.tensor_tensor(w2l[:, bass.ds(s * F, F)], w2_stage[:], w2h[:, bass.ds(s * F, F)],
                                       ALU.subtract).then_inc(pool_w, 1)
                b = s + 2
                if has(b):
                    pool.wait_ge(act_qk, count(b, 1))
                    if peeled(b) and b == 0:
                        pool.wait_ge(tables_ready, 1)
                    for i, (dst, table) in enumerate(((qks, sin8), (qk, cos8))):
                        for j in range(2):
                            tab = table[:, bass.ds(b * HD, HD)].rearrange("p (a d) -> p a d", a=1).to_broadcast([P, H, HD])
                            pool.tensor_tensor(dst[:, j, :].rearrange("p (h d) -> p h d", d=HD),
                                               qk[:, j, :].rearrange("p (h d) -> p h d", d=HD), tab, ALU.mult).then_inc(pool_mul, 1)
                    pool.wait_ge(pool_mul, count(b, 4))
                    pairs_c = qk[:].rearrange("p i (n e) -> p (i n) e", e=2)
                    pairs_s = qks[:].rearrange("p i (n e) -> p (i n) e", e=2)
                    pool.tensor_tensor(pairs_c[:, :, 0], pairs_c[:, :, 0], pairs_s[:, :, 1], ALU.add)
                    pool.tensor_tensor(pairs_c[:, :, 1], pairs_c[:, :, 1], pairs_s[:, :, 0], ALU.add).then_inc(pool_rope, 1)
                b = s - 2
                if has(b):
                    pool.wait_ge(act_x2hi, count(b, 1))
                    pool.tensor_tensor(x2[:, par, D:2 * D], x2f[:], x2[:, par, 0:D],
                                       ALU.subtract).then_inc(pool_x2lo, 1)
                if has(s + 2):
                    add_bias(s + 2)

            pool.wait_ge(small_loaded, 16 * (5 + UNITS))
            run_steps(pool, step)

        @block.scalar
        def _(act):
            act.wait_ge(setup_v, 11)
            act.activation(sincos[:], ang[:], ACT.Sin).then_inc(setup_a, 1)

            def exp_unit(b, u):
                act.wait_ge(pe_st, count(b, UNITS, u + 1))
                if not peeled(b) or b * UNITS + u >= NPB:
                    act.wait_ge(pe_av, count(b, UNITS, u + 1 - NPB))
                act.activation(probs[u % NPB][:], t_bank[u % 2][:], ACT.Exp, scale=EXP_SCALE).then_inc(act_exp, 1)

            def split_weights(s, k):
                stage, hi, ready = ((w1_stage, w1h, 1), (w2_stage, w2h, 2))[k]
                act.wait_ge(dve_ws, count(s, 2, ready))
                act.copy(hi[:, bass.ds(s * F, F)], stage[:]).then_inc(act_w, 1)

            def step(s, par):
                def values(k):
                    act.wait_ge(pe_av, count(s - 1, UNITS, (k + 1) * HALF))
                    if not peeled(s - 1) or s - 1 >= 1:
                        act.wait_ge(pe_oT, count(s - 2, 2, k + 1))
                    act.copy(o_sb[k][:], o_bank[:]).then_inc(act_o, 1)

                for u in range(UNITS):
                    if has(s - 1):
                        exp_unit(s - 1, u)
                    if u == HALF and has(s - 1):
                        values(0)
                    if u == 0 and has(s - 3):
                        b = s - 3
                        act.wait_ge(pe_x2T, count(b, 1))
                        act.wait_ge(pe_out, count(b, 1))
                        act.mul(turned[:], m0[:, 0:D].rearrange("p (c t) -> p c t", c=DC), 1.0 / XS).then_inc(act_x2T, 1)
                    if u == 1 and has(s - 2):
                        b = s - 2
                        act.wait_ge(pe_attnT, count(b, 1))
                        if has(b - 1):
                            act.wait_ge(pe_gate, count(b - 1, 1))
                        act.copy(turned[:], m2[:, 0:D].rearrange("p (c t) -> p c t", c=DC)).then_inc(act_attnT, 1)
                    if u == 1 and has(s):
                        act.wait_ge(pe_v, count(s, 1))
                        if not peeled(s) or s >= 2:
                            act.wait_ge(pe_av, count(s - 2, UNITS))
                        if peeled(s) and s == 0:
                            act.wait_ge(slots_ready, 1)
                        act.copy(v[par][:, :, 0:HD], m1[:, 0:D].rearrange("p (h d) -> p h d", d=HD)).then_inc(act_v, 1)
                    if u == 2 and has(s + 1):
                        b = s + 1
                        act.wait_ge(pool_rope, count(b, 1))
                        if peeled(b) and b == 0:
                            act.wait_ge(slots_ready, 1)
                        if not peeled(b) or b >= 1:
                            act.wait_ge(pe_tk, count(b - 1, 1))
                        if not peeled(b) or b >= 2:
                            act.wait_ge(pe_tq2, count(b - 2, 1))
                        q4 = qx[1 - par][:].rearrange("p h (k d) -> p h k d", d=HD)
                        k4 = kx[:].rearrange("p h (k d) -> p h k d", d=HD)
                        qr = qk[:, 0, :].rearrange("p (h a d) -> p h a d", a=1, d=HD).to_broadcast([P, H, 2, HD])
                        kr = qk[:, 1, :].rearrange("p (h a d) -> p h a d", a=1, d=HD).to_broadcast([P, H, 2, HD])
                        act.copy(q4[:, :, 0:2, :], qr)
                        act.copy(k4[:, :, 0:4:2, :], kr).then_inc(act_hi, 1)
                    if u == 3 and has(s + 2):
                        b = s + 2
                        act.wait_ge(pe_xT, count(b, 1))
                        if not peeled(b) or b >= 1:
                            act.wait_ge(pe_qk, count(b - 1, 1))
                        act.copy(xT[:], m0[:, 0:D].rearrange("p (c t) -> p c t", c=DC))
                        if not peeled(b) or b >= 2:
                            act.wait_ge(pe_v, count(b - 2, 1))
                        act.copy(ctxT[par][:], m0[:, D:D + P]).then_inc(act_xT, 1)
                    if u in (3, 5) and has(s):
                        split_weights(s, (u - 3) // 2)
                    if u == 4 and has(s - 2):
                        b = s - 2
                        act.wait_ge(dve_x1, count(b, 1))
                        act.copy(x1[:, bass.ds(b * D, D)], x1b[:]).then_inc(act_x1, 1)
                    if u == 6 and has(s + 2):
                        b = s + 2
                        act.wait_ge(pe_qk, count(b, 1))
                        if not peeled(b) or b >= 1:
                            act.wait_ge(pool_lo, count(b - 1, 1))
                        act.copy(qk[:], m1[:].rearrange("p (i d) -> p i d", i=2)).then_inc(act_qk, 1)
                    if u == 7 and has(s - 2):
                        b = s - 2
                        act.wait_ge(dve_x2, count(b, 1))
                        if not peeled(b) or b >= 2:
                            act.wait_ge(x2_stored[par], paired(b - 2, par))
                        act.copy(x2[:, par, 0:D], x2f[:]).then_inc(act_x2hi, 1)
                if has(s + 1):
                    b = s + 1
                    act.wait_ge(pe_tk, count(b, 1))
                    if not peeled(b) or b >= 2:
                        act.wait_ge(pe_st, count(b - 2, UNITS))
                    act.copy(kT[1 - par][:], tk_16.rearrange("p (g t) -> p g t", g=HG)).then_inc(act_tk, 1)
                if has(s - 1):
                    values(1)

            run_steps(act, step)

        @block.vector
        def _(dve):
            n = [0]

            def chain(ins):
                n[0] += 1
                ins.then_inc(setup_v, 1)
                dve.wait_ge(setup_v, n[0])

            dve.wait_ge(pos_loaded, 16)
            a4 = ang[:, 0, :].rearrange("p (n j) -> p n j", j=2)
            flat = pos_sb[:].rearrange("p b c -> p (b c)")
            for j in range(2):
                chain(dve.tensor_scalar(a4[:, :, j], flat, float(np.float32(10000.0 ** (-j / 2))), None, ALU.mult))
            chain(dve.tensor_scalar(ang[:, 1, :], ang[:, 0, :], math.pi / 2, None, ALU.add))
            chain(dve.tensor_scalar(turns_i[:], ang[:], 1.0 / TWO_PI, None, ALU.mult))
            chain(dve.tensor_copy(turns[:], turns_i[:]))
            chain(dve.scalar_tensor_tensor(ang[:], turns[:], -TWO_PI, ang[:], ALU.mult, ALU.add))
            for sign, cmp in ((-1.0, ALU.is_gt), (1.0, ALU.is_lt)):
                chain(dve.tensor_scalar(turns[:], ang[:], -sign * math.pi, sign * TWO_PI, cmp, ALU.mult))
                chain(dve.tensor_tensor(ang[:], ang[:], turns[:], ALU.add))
            chain(dve.tensor_scalar(ang[:], ang[:], math.pi, -math.pi, ALU.min, ALU.max))
            def statistics(lo, hi):
                for b in range(lo, hi):
                    n[0] += 1
                    dve.bn_stats(bn1[:, b * 6:(b + 1) * 6], x1[:, b * D:(b + 1) * D]).then_inc(setup_v, 1)
                for b in range(lo, hi):
                    dve.wait_ge(setup_v, n[0] - (hi - 1 - b))
                    dve.bn_aggr(mv1[:, b * 2:b * 2 + 2], bn1[:, b * 6:(b + 1) * 6]).then_inc(stats1_ready, 1)
                dve.wait_ge(stats1_ready, hi)
                var = mv1[:].rearrange("p (b k) -> p b k", k=2)[:, lo:hi, 1]
                rsqrt(dve, var, rs1[:, lo:hi], nt1[:, :, lo:hi], nt1i[:, lo:hi], setup_v, n[0])
                n[0] += RSQRT_OPS

            dve.wait_ge(x_loaded, 16)
            statistics(0, FIRST)
            dve.wait_ge(setup_a, 1)
            c2 = cos8[:].rearrange("p (n e) -> p n e", e=2)
            s2 = sin8[:].rearrange("p (n e) -> p n e", e=2)
            dve.tensor_scalar(c2[:, :, 0], sincos[:, 1, :], QS, None, ALU.mult)
            dve.tensor_scalar(c2[:, :, 1], sincos[:, 1, :], QS, None, ALU.mult)
            dve.tensor_scalar(s2[:, :, 0], sincos[:, 0, :], QS, None, ALU.mult)
            dve.tensor_scalar(s2[:, :, 1], sincos[:, 0, :], -QS, None, ALU.mult).then_inc(tables_ready, 1)

            def normalize(b):
                dve.tensor_scalar(xhat[:], x1[:, bass.ds(b * D, D)], mv1[:, bass.ds(b * 2, 1)], rs1[:, bass.ds(b, 1)],
                                  ALU.subtract, ALU.mult).then_inc(dve_xhat, 1)

            def refine(b, k, y):
                var, a, p = nt2[:, 0:1], nt2[:, 1:2], nt2[:, 2:3]
                steps = ((a, var, y, y, ALU.mult, ALU.mult), (p, a, 3.0 / 8, -10.0 / 8, ALU.mult, ALU.add),
                         (p, p, a, 15.0 / 8, ALU.mult, ALU.add), (rs2[:], p, y, (1.0, XS)[k], ALU.mult, ALU.mult))
                for i, args in enumerate(steps):
                    dve.tensor_scalar(*args).then_inc(dve_chain, 1)
                    dve.wait_ge(dve_chain, count(b, CHAIN2, 3 + 4 * k + i + 1))

            def first_guess(b):
                dve.tensor_scalar(nt2[:, 0:1], mv2[:, 1:2], EPS, None, ALU.add).then_inc(dve_chain, 1)
                dve.wait_ge(dve_chain, count(b, CHAIN2, 1))
                dve.tensor_copy(nt2[:, 1:2], nt2[:, 0:1].bitcast(I32)).then_inc(dve_chain, 1)
                dve.wait_ge(dve_chain, count(b, CHAIN2, 2))
                dve.tensor_scalar(nt2i[:], nt2[:, 1:2], -0.5, RSQRT_MAGIC, ALU.mult, ALU.add).then_inc(dve_chain, 1)
                dve.wait_ge(dve_chain, count(b, CHAIN2, 3))

            mx_units = mx[:].rearrange("p (k g j) -> p k g j", k=2, j=ROWT)

            def divide(b, k):
                oT = m2[:].rearrange("p (n c) -> p n c", c=VW)
                dve.wait_ge(pe_oT, count(b, 2, k + 1))
                dve.reciprocal(recip[:], oT[:, :, HD]).then_inc(dve_rec, 1)
                dve.wait_ge(dve_rec, count(b, 2, k + 1))
                if k == 0 and (not peeled(b) or b >= 1):
                    dve.wait_ge(pe_attnT, count(b - 1, 1))
                dve.tensor_tensor(attn[:, k * P:(k + 1) * P].rearrange("p (n d) -> p n d", d=HD), oT[:, :, 0:HD],
                                  recip[:].rearrange("p (n a) -> p n a", a=1).to_broadcast([P, HALF * UH, HD]),
                                  ALU.mult).then_inc(dve_norm, 1)

            def step(s, par):
                for u in range(UNITS):
                    if u == 4 and has(s - 2):
                        dve.wait_ge(dve_bn, count(s - 2, 1))
                    if has(s):
                        dve.wait_ge(pe_s, count(s, UNITS, u + 1))
                        if u == 0 and (not peeled(s) or s >= 1):
                            dve.wait_ge(dve_m, count(s - 1, 1))
                        dve.tensor_reduce(mx_units[:, u % 2, :, u // 2],
                                          s_bank[u % 2][:].rearrange("p (h k) -> p h k", k=P),
                                          AX.X, ALU.max).then_inc(dve_max, 1)
                    if u == 2 and has(s - 3):
                        b = s - 3
                        dve.wait_ge(pe_gate, count(b, 1))
                        dve.tensor_tensor(logits[:, bass.ds(b, 1), :].rearrange("p a e -> p (a e)"), m0[:, D:D + E], gb_bc[:], ALU.add).then_inc(dve_gate, 1)
                    if u == 3 and has(s - 2):
                        b = s - 2
                        dve.wait_ge(pe_out, count(b, 1))
                        dve.wait_ge(pool_xb, count(b, 1))
                        if not peeled(b) or b >= 1:
                            dve.wait_ge(act_x1, count(b - 1, 1))
                        dve.tensor_tensor(x1b[:], m2[:, D:2 * D], x1[:, bass.ds(b * D, D)], ALU.add).then_inc(dve_x1, 1)
                        dve.wait_ge(dve_x1, count(b, 1))
                        dve.bn_stats(bn2[:], x1b[:]).then_inc(dve_bn, 1)
                    if u == 4 and has(s - 2):
                        dve.bn_aggr(mv2[:], bn2[:]).then_inc(dve_stats, 1)
                    if u == 5 and has(s - 2):
                        dve.wait_ge(dve_stats, count(s - 2, 1))
                        first_guess(s - 2)
                        refine(s - 2, 0, nt2i[:].bitcast(F32))
                    if u == 6 and has(s - 2):
                        b = s - 2
                        refine(b, 1, rs2[:])
                        if not peeled(b) or b >= 1:
                            dve.wait_ge(pe_x2T, count(b - 1, 1))
                            dve.wait_ge(pool_x2lo, count(b - 1, 1))
                        dve.tensor_scalar(x2f[:], x1b[:], mv2[:, 0:1], rs2[:],
                                          ALU.subtract, ALU.mult).then_inc(dve_x2, 1)
                    if u == 0 and has(s - 2):
                        divide(s - 2, 1)
                    if u == 1 and has(s + 2):
                        if has(s + 1):
                            dve.wait_ge(pe_xT, count(s + 1, 1))
                        normalize(s + 2)
                    if u == 1 and peeled(s) and s == -1:
                        dve.wait_ge(x_rest_loaded, 16)
                        statistics(FIRST, B)
                    if u in (1, 3) and has(s):
                        stage, loaded = ((w1_stage, w1_loaded), (w2_stage, w2_loaded))[u // 2]
                        dve.wait_ge(loaded, count(s, 16))
                        dve.tensor_scalar(stage[:], stage[:], WS, None, ALU.mult).then_inc(dve_ws, 1)
                if has(s):
                    dve.wait_ge(dve_max, count(s, UNITS))
                    dve.tensor_scalar(qx[par][:, :, MROW], mx[:], -1.0 / QS, None, ALU.mult).then_inc(dve_m, 1)
                if has(s - 1):
                    divide(s - 1, 0)
                if has(s + 1):
                    dve.wait_ge(pe_tq1, count(s + 1, 1))
                    if has(s - 1):
                        dve.wait_ge(pe_st, count(s - 1, UNITS))
                    dve.tensor_copy(qT[1 - par][:], tq1_16.rearrange("p (g t) -> p g t", g=HG)).then_inc(dve_tq1, 1)
                if has(s):
                    dve.wait_ge(pe_tq2, count(s, 1))
                    dve.tensor_copy(qT[par][:], tq2_16.rearrange("p (g t) -> p g t", g=HG)).then_inc(dve_tq2, 1)

            run_steps(dve, step)

        @block.tensor
        def _(pe):
            pe.wait_ge(consts_ready, 1)
            pe.wait_ge(small_loaded, 16 * (5 + UNITS))

            def pack_T(dst, src, done):
                for g in range(HG):
                    last = pe.transpose(dst[:, g * P:(g + 1) * P],
                                        src[:, g * ROWT:(g + 1) * ROWT, :].rearrange("p h d -> p (h d)"), ident16[:])
                last.then_inc(done, 1)

            def av(b, par, u):
                pe.wait_ge(act_exp, count(b, UNITS, u + 1))
                if u == 0:
                    pe.wait_ge(act_v, count(b, 1))
                if u % HALF == 0:
                    k = u // HALF
                    if not peeled(b) or b >= 1 or k == 1:
                        pe.wait_ge(act_o, count(b, 2, k))
                for i in range(UH):
                    h = ((u % 2) * UH + i) * ROWT + u // 2
                    last = pe.matmul(o_bank[SLOT * i:SLOT * (i + 1), (u % HALF) * P:(u % HALF + 1) * P],
                                     v[par][:, h, :], probs[u % NPB][:, i * P:(i + 1) * P], start=True, stop=True)
                last.then_inc(pe_av, 1)

            def turn_values(b, k):
                pe.wait_ge(act_o, count(b, 2, k + 1))
                for n in range(HALF):
                    last = pe.transpose(m2[:, n * P:(n + 1) * P], o_sb[k][:, n * P:(n + 1) * P], ident[:])
                last.then_inc(pe_oT, 1)

            def scores(out_bank, stat, mov, rows, u, done):
                j = u // 2
                for i in range(UH):
                    g = (u % 2) * UH + i
                    last = pe.matmul(out_bank[:, i * P:(i + 1) * P], stat[SLOT * j:SLOT * j + rows, g, :],
                                     mov[SLOT * j:SLOT * j + rows, g, :], start=True, stop=True)
                last.then_inc(done, 1)

            def score_unit(s, par, u):
                if u == 0:
                    pe.wait_ge(dve_tq1, count(s, 1))
                    pe.wait_ge(act_tk, count(s, 1))
                if not peeled(s) or s * UNITS + u >= 2:
                    pe.wait_ge(dve_max, count(s, UNITS, u - 1))
                scores(s_bank[u % 2], qT[par], kT[par], MROW, u, pe_s)

            def step(s, par):
                if has(s):
                    score_unit(s, par, 0)
                for u in range(UNITS):
                    if u < UNITS - 1 and has(s):
                        if u == 0 and has(s - 1):
                            pe.wait_ge(dve_tq2, count(s - 1, 1))
                        score_unit(s, par, u + 1)
                    if has(s - 1):
                        b = s - 1
                        if u == 0:
                            pe.wait_ge(dve_tq2, count(b, 1))
                        if not peeled(b) or b * UNITS + u >= 2:
                            pe.wait_ge(act_exp, count(b, UNITS, u - 1))
                        scores(t_bank[u % 2], kT[1 - par], qT[1 - par], SLOT, u, pe_st)
                    if u == UNITS - 1 and has(s + 1):
                        pe.wait_ge(pool_lo, count(s + 1, 1))
                        if has(s):
                            pe.wait_ge(dve_max, count(s, UNITS, UNITS - 1))
                        pack_T(tk_16, kx, pe_tk)
                    if has(s - 1) and u >= 1:
                        av(s - 1, 1 - par, u - 1)
                    if u == 0 and has(s - 2):
                        pe.wait_ge(dve_norm, count(s - 2, 2, 1))
                        turn_values(s - 2, 1)
                    if u == 0 and has(s - 3):
                        b = s - 3
                        pe.wait_ge(dve_x2, count(b, 1))
                        if not has(s):
                            pe.wait_ge(dve_gate, count(b - 1, 1))
                        for c in range(DC):
                            last = pe.transpose(m0[:, c * P:(c + 1) * P], x2f[:, c * P:(c + 1) * P], ident[:])
                        last.then_inc(pe_x2T, 1)
                    if u == 1 and has(s - 2):
                        pe.wait_ge(dve_norm, count(s - 2, 2))
                        for c in range(DC):
                            last = pe.transpose(m2[:, c * P:(c + 1) * P], attn[:, c * P:(c + 1) * P], ident[:])
                        last.then_inc(pe_attnT, 1)
                    if u == 1 and has(s - 3):
                        pe.wait_ge(act_x2T, count(s - 3, 1))
                        for c in range(DC):
                            last = pe.matmul(m0[:, D:D + E], turned[:, c, :], gw_sb[:, c, :], start=(c == 0), stop=(c == DC - 1))
                        last.then_inc(pe_gate, 1)
                    if u == 2 and has(s - 2):
                        pe.wait_ge(act_attnT, count(s - 2, 1))
                        for c in range(DC):
                            last = pe.matmul(m2[:, D:2 * D], turned[:, c, :], wout_sb[:, c, :], start=(c == 0), stop=(c == DC - 1))
                        last.then_inc(pe_out, 1)
                    if u == 3 and has(s + 2):
                        b = s + 2
                        pe.wait_ge(dve_xhat, count(b, 1))
                        pe.wait_ge(ctx_loaded[par], paired(b, par))
                        if has(s - 3):
                            pe.wait_ge(dve_gate, count(s - 3, 1))
                        elif has(s):
                            pe.wait_ge(dve_tq1, count(s, 1))
                        elif has(s + 1):
                            pe.wait_ge(act_xT, count(s + 1, 1))
                        for c in range(DC):
                            pe.transpose(m0[:, c * P:(c + 1) * P], xhat[:, c * P:(c + 1) * P], ident[:])
                        pe.transpose(m0[:, DC * P:(DC + 1) * P], ctx_sb[:, par, :], ident[:]).then_inc(pe_xT, 1)
                    if u == 4 and has(s + 2):
                        pe.wait_ge(act_xT, count(s + 2, 1))
                        if has(s):
                            pe.wait_ge(act_v, count(s, 1))
                        elif has(s + 1):
                            pe.wait_ge(act_qk, count(s + 1, 1))
                        for c in range(DC):
                            pe.matmul(m1[:, 0:D], xT[:, c, :], wq_sb[:, c, :], start=(c == 0), stop=(c == DC - 1))
                    if u == 5 and has(s + 2):
                        pe.matmul(m1[:, D:2 * D], ctxT[par][:], wkv_sb[:, 0:D], start=True, stop=True).then_inc(pe_qk, 1)
                    if u == 6 and has(s - 1):
                        if has(s - 2):
                            pe.wait_ge(act_attnT, count(s - 2, 1))
                            pe.wait_ge(dve_x1, count(s - 2, 1))
                        turn_values(s - 1, 0)
                    if u == UNITS - 1 and has(s + 1):
                        if has(s + 2):
                            pe.wait_ge(act_qk, count(s + 2, 1))
                        else:
                            pe.wait_ge(act_v, count(s, 1))
                        pe.matmul(m1[:, 0:D], ctxT[1 - par][:], wkv_sb[:, D:2 * D], start=True, stop=True).then_inc(pe_v, 1)
                        if has(s + 2):
                            pe.wait_ge(act_xT, count(s + 2, 1))
                        else:
                            pe.wait_ge(dve_gate, count(s - 3, 1))
                        pack_T(tq1_16, qx[1 - par], pe_tq1)
                if has(s - 1):
                    av(s - 1, 1 - par, UNITS - 1)
                if has(s):
                    pe.wait_ge(dve_m, count(s, 1))
                    pack_T(tq2_16, qx[par], pe_tq2)

            run_steps(pe, step)


def experts(nc, b1, b2, out, x1, logits, w1h, w1l, w2h, w2l, ident, ident16, x2_dram, y_dram):
    with ExitStack() as ctx:
        def sb(name, shape, dt):
            return ctx.enter_context(nc.sbuf_tensor(name, shape, dt))

        def bank(name, shape, dt):
            return ctx.enter_context(nc.psum_tensor(name, shape, dt))

        def sem(name):
            return ctx.enter_context(nc.semaphore(name))

        LAP = 6
        KT = 16
        below = sb("below", [P, P], F32)
        ones = sb("ones", [P, P], F32)
        iota_i = sb("iota_i", [P, P], I32)
        iota_f = sb("iota_f", [P, P], F32)
        mark_i = sb("mark_i", [P, B], I32)
        marks = sb("marks", [P, 2, B], F32)
        pad_i = sb("pad_i", [P, TILES], I32)
        pad_rows = sb("pad_rows", [P, TILES], F32)
        b1_rows = sb("b1_rows", [E * FC, P], F32)
        b1T = sb("b1T", [P, E * FC], F32)
        b2_bc = sb("b2_bc", [P, E * D], F32)
        prob = sb("prob", [P, B, E], F32)
        prob2 = sb("prob2", [P, B, E], F32)
        cand = sb("cand", [P, B, E], F32)
        first = sb("first", [P, B, E], F32)
        second = sb("second", [P, B, E], F32)
        chosen = sb("chosen", [P, B, E], F32)
        run = [sb(f"run{i}", [P, B, E], F32) for i in range(2)]
        slot_of = sb("slot_of", [P, B, E], F32)
        top = sb("top", [P, B], F32)
        top1 = sb("top1", [P, B], F32)
        top2 = sb("top2", [P, B], F32)
        norm = sb("norm", [P, B], F32)
        weight = [sb(f"weight{i}", [P, B], F32) for i in range(2)]
        slot_f = sb("slot_f", [P, 2, B], F32)
        slot_i = sb("slot_i", [P, 2, B], I32)
        place_i = sb("place_i", [P, 2, B], I32)
        place = sb("place", [P, 2, B], F32)
        tile_of = sb("tile_of", [P, 2, B], F32)
        tile_hot = sb("tile_hot", [P, 2, B, TILES], F16)
        place_hot = sb("place_hot", [P, 2, B, P], F16)
        over = sb("over", [P, E, KT], F32)
        tiles = [sb(f"tiles{i}", [P, E], F32) for i in range(3)]
        past = sb("past", [1, TILES + 1, E], F32)
        tile_f = sb("tile_f", [1, TILES + 1], F32)
        w_at = sb("w_at", [1, TILES + 1], I32)
        b1_at = sb("b1_at", [1, TILES + 1], I32)
        b2_at = sb("b2_at", [1, TILES + 1], I32)
        slot_mark = sb("slot_mark", [P, TILES], F32)
        slot_token = sb("slot_token", [P, TILES], F32)
        slot_row = sb("slot_row", [P, TILES], F32)
        slot_pad = sb("slot_pad", [P, TILES], F32)
        token_ids = sb("token_ids", [P, TILES], I32)
        row_ids = sb("row_ids", [P, TILES], I32)
        spare = sb("spare", [P, 1], F32)
        tile_tokens = [sb(f"tile_tokens{i}", [P, 1], I32) for i in range(2)]
        tile_rows = [sb(f"tile_rows{i}", [P, 1], I32) for i in range(2)]
        xg = [sb(f"xg{i}", [P, 2 * D], F16) for i in range(2)]
        xgT = [sb(f"xgT{i}", [P, 2 * DC, P], F16) for i in range(2)]
        h = [sb(f"h{i}", [P, FC * P], F32) for i in range(2)]
        hh = [sb(f"hh{i}", [P, FC * P], F16) for i in range(2)]
        hl = [sb(f"hl{i}", [P, FC * P], F16) for i in range(2)]
        y = [sb(f"y{i}", [P, D], F32) for i in range(2)]
        QB = B // 4
        yq = [place_hot[:].rearrange("p k b q -> p (k b q)").bitcast(F32).rearrange("p (k b d) -> p k b d", k=2, b=QB),
              sb("yq1", [P, 2, QB, D], F32)]

        h_bank = [bank(f"h_bank{i}", [P, 512], F32) for i in range(4)]
        x_bank = bank("x_bank", [P, 1024], F16)
        y_bank = [bank(f"y_bank{i}", [P, 512], F32) for i in range(2)]
        r_bank = bank("r_bank", [P, 512], F32)

        names = """consts ranks_in loaded shifted exp_ready routed ranks_ready tile_eq_ready b1_ready
        tile_hot_ready place_hot_ready marks_in ids_ready pe_b1 table_ready pool_hot pool_tokens pool_rows
        pe_x pe_h pe_y dve_x dve_hi dve_lo dve_y act_h combined stored""".split()
        sems = {n: sem("e_" + n) for n in names}
        (consts, ranks_in, loaded, shifted, exp_ready, routed, ranks_ready, tile_eq_ready, b1_ready,
         tile_hot_ready, place_hot_ready, marks_in, ids_ready, pe_b1, table_ready, pool_hot, pool_tokens, pool_rows,
         pe_x, pe_h, pe_y, dve_x, dve_hi, dve_lo, dve_y, act_h, combined, stored) = [sems[n] for n in names]
        x_gathered = [sem(f"x_gathered{i}") for i in range(2)]
        y_scattered = [sem(f"y_scattered{i}") for i in range(2)]
        y_loaded = [sem(f"y_loaded{i}") for i in range(2)]
        CONSTS = 8

        def shared(i, par):
            return 8 * i + (16 if par == 0 else 8)

        def within(i):
            return not isinstance(i, int) or 0 <= i < TILES

        def run_tiles(eng, step, engine=None, table=None, most=0):
            def numbers(i, n):
                if table is None:
                    return [None] * n
                _, values = nc.values_load_multi_w_load_instructions(
                    table[0:1, bass.ds(i, n)], engines=[engine], min_val=0, max_val=most,
                    skip_runtime_bounds_check_because="the tables hold a count of experts, from 0 and cut at E-1, times a size")
                return list(values)

            at = [None] * 3 + numbers(0, LAP + 1)
            for i in range(-3, LAP):
                step(i, i % 2, at[i + 3:i + 5])
            with eng.Fori(1, (TILES - 3) // LAP) as lap:
                at = numbers(LAP * lap, LAP + 1)
                for i in range(LAP):
                    step(LAP * lap + i, i % 2, at[i:i + 2])
            at = numbers(TILES - 3, 4)
            for i in range(3):
                step(TILES - 3 + i, (TILES - 3 + i) % 2, at[i:i + 2])

        def bc(ap, shape, at):
            s = {1: "p (a n) -> p a n", 2: "p (n a) -> p n a"}[at]
            return ap.rearrange(s, a=1).to_broadcast(shape)

        block = ctx.enter_context(nc.Block())

        @block.sync
        def _(sp):
            sp.dma_start(b1_rows[:], b1.rearrange("e (c p) -> (e c) p", p=P)).then_inc(loaded, 16)
            sp.dma_start(b2_bc[:], b2.rearrange("(a e) d -> a (e d)", a=1).to_broadcast([P, E * D])).then_inc(loaded, 16)
            for i in range(2):
                sp.wait_ge(y_scattered[i], 16 * ((TILES + 1 - i) // 2))
            rows = y_dram[0:2 * B * P, :].rearrange("(k b p) d -> k p b d", k=2, p=P)
            for q in range(B // QB):
                if q >= 2:
                    sp.wait_ge(combined, (q - 1) * QB)
                for k in range(2):
                    sp.dma_start(yq[q % 2][:, k], rows[k, :, q * QB:(q + 1) * QB]).then_inc(y_loaded[q % 2], 16)

        @block.gpsimd
        def _(pool):
            pool.memset(ones[:], 1.0).then_inc(consts, 1)
            pool.iota(iota_i[:], pattern=[[1, P]], base=0, channel_multiplier=0).then_inc(consts, 1)
            pool.iota(mark_i[:], pattern=[[P, B]], base=1, channel_multiplier=1).then_inc(consts, 1)
            pool.iota(pad_i[:], pattern=[[P, TILES]], base=2 * B * P, channel_multiplier=1).then_inc(consts, 1)
            pool.wait_ge(consts, 4)
            pool.affine_select(out=below[:], in_=ones[:], compare_op=ALU.is_gt, fill=0.0, base=0,
                               pattern=[[1, P]], channel_multiplier=-1).then_inc(consts, 1)
            pool.tensor_copy(iota_f[:], iota_i[:]).then_inc(consts, 1)
            pool.tensor_copy(pad_rows[:], pad_i[:]).then_inc(consts, 1)
            pool.tensor_copy(marks[:, 0, :], mark_i[:]).then_inc(consts, 1)
            pool.wait_ge(consts, CONSTS)
            pool.tensor_scalar(marks[:, 1, :], marks[:, 0, :], -1.0, None, ALU.mult).then_inc(pool_hot, 1)
            pool.wait_ge(pool_hot, 1)
            for k in range(2):
                pool.wait_ge(tile_eq_ready, k + 1)
                pool.tensor_tensor(tile_hot[:, k], tile_hot[:, k], bc(marks[:, k, :], [P, B, TILES], 2), ALU.mult).then_inc(tile_hot_ready, 1)

            def column(dst, ids, i, done):
                pool.wait_ge(consts, CONSTS)
                pool.tensor_copy(dst[:], ids[:, bass.ds(i, 1)]).then_inc(done, 1)
                pool.wait_ge(done, i + 1)
                if not isinstance(i, int):
                    pool.tensor_tensor(spare[:], ones[:, 0:1], ones[:, 0:1], ALU.mult)

            pool.wait_ge(ids_ready, 1)

            def step(i, par, _):
                if within(i + 3):
                    t = i + 3
                    tp = 1 - par
                    if not isinstance(i, int) or t >= 2:
                        pool.wait_ge(pe_x, t - 1)
                    column(tile_tokens[tp], token_ids, t, pool_tokens)
                    pool.indirect_dma_start(out=xg[tp][:], out_offset=None, in_=x2_dram,
                                            in_offset=bass.IndirectOffsetOnAxis(ap=tile_tokens[tp][:], axis=0)).then_inc(x_gathered[tp], 16)
                if within(i):
                    if not isinstance(i, int) or i >= 2:
                        pool.wait_ge(y_scattered[par], shared(i - 2, par))
                    pool.wait_ge(dve_y, i + 1)
                    column(tile_rows[par], row_ids, i, pool_rows)
                    pool.indirect_dma_start(out=y_dram, out_offset=bass.IndirectOffsetOnAxis(ap=tile_rows[par][:], axis=0),
                                            in_=y[par][:], in_offset=None).then_inc(y_scattered[par], 16)

            run_tiles(pool, step)

        @block.scalar
        def _(act):
            act.wait_ge(shifted, 1)
            act.activation(prob[:], prob[:], ACT.Exp).then_inc(exp_ready, 1)
            act.wait_ge(table_ready, 3)
            act.wait_ge(b1_ready, 1)

            def step(i, par, at):
                if not within(i + 1):
                    return
                t = i + 1
                for k in range(2):
                    act.wait_ge(pe_h, count(t, 2, k + 1))
                    if not isinstance(t, int) or t >= 2:
                        act.wait_ge(dve_lo, count(t - 2, 2, k + 1))
                    for c in range(4):
                        f = 4 * k + c
                        last = act.activation(h[1 - par][:, f * P:(f + 1) * P], h_bank[2 * (1 - par) + k][:, c * P:(c + 1) * P],
                                              ACT.Gelu_apprx_tanh, bias=b1T[:, bass.ds(at[1] + f, 1)], scale=1.0 / (XS * WS))
                    last.then_inc(act_h, 1)

            run_tiles(act, step, mybir.EngineType.Activation, b1_at, (E - 1) * FC)
            for b in range(B):
                act.wait_ge(combined, b + 1)
                act.dma_start(out[b], x1[:, b * D:(b + 1) * D]).then_inc(stored, 16)
            act.wait_ge(stored, 16 * B)

        @block.vector
        def _(dve):
            n = [0]

            def chain(ins):
                n[0] += 1
                ins.then_inc(routed, 1)
                dve.wait_ge(routed, n[0])

            full = [P, B, E]
            chain(dve.tensor_reduce(top[:], logits[:], AX.X, ALU.max))
            dve.tensor_tensor(prob[:], logits[:], bc(top[:], full, 2), ALU.subtract).then_inc(shifted, 1)
            dve.wait_ge(exp_ready, 1)
            chain(dve.tensor_reduce(norm[:], prob[:], AX.X, ALU.add))
            chain(dve.reciprocal(norm[:], norm[:]))
            chain(dve.tensor_tensor(prob[:], prob[:], bc(norm[:], full, 2), ALU.mult))
            dve.wait_ge(consts, CONSTS)
            experts_iota = iota_f[:, 0:E].rearrange("p (a e) -> p a e", a=1).to_broadcast(full)

            def best(p, value, mask):
                chain(dve.tensor_reduce(value[:], p[:], AX.X, ALU.max))
                chain(dve.tensor_tensor(cand[:], p[:], bc(value[:], full, 2), ALU.is_equal))
                chain(dve.scalar_tensor_tensor(cand[:], cand[:], -float(E), experts_iota, ALU.mult, ALU.add))
                chain(dve.tensor_reduce(norm[:], cand[:], AX.X, ALU.min))
                chain(dve.tensor_tensor(mask[:], cand[:], bc(norm[:], full, 2), ALU.is_equal))

            best(prob, top1, first)
            chain(dve.scalar_tensor_tensor(prob2[:], first[:], -2.0, prob[:], ALU.mult, ALU.add))
            best(prob2, top2, second)
            dve.tensor_tensor(chosen[:], first[:], second[:], ALU.add).then_inc(ranks_in, 1)
            chain(dve.tensor_tensor(norm[:], top1[:], top2[:], ALU.add))
            chain(dve.reciprocal(norm[:], norm[:]))
            dve.tensor_tensor(weight[0][:], top1[:], norm[:], ALU.mult)
            chain(dve.tensor_tensor(weight[1][:], top2[:], norm[:], ALU.mult))
            dve.wait_ge(ranks_ready, 1)
            ranks = r_bank[:, 0:P].rearrange("p (b e) -> p b e", e=E)
            totals = r_bank[:, P:2 * P].rearrange("p (b e) -> p b e", e=E)
            dve.memset(run[0][:, 0:1, :], 0.0)
            chain(dve.tensor_copy(run[0][:, 1:B, :], totals[:, 0:B - 1, :]))
            src = 0
            for d in (1, 2, 4, 8):
                a, z = run[src], run[1 - src]
                dve.tensor_copy(z[:, 0:d, :], a[:, 0:d, :])
                chain(dve.tensor_tensor(z[:, d:B, :], a[:, d:B, :], a[:, 0:B - d, :], ALU.add))
                src = 1 - src
            before = run[src]
            chain(dve.tensor_tensor(top[:, 0:E], totals[:, B - 1, :], before[:, B - 1, :], ALU.add))
            thresholds = iota_f[:, 0:KT].rearrange("p (a k) -> p a k", a=1).to_broadcast([P, E, KT])
            chain(dve.tensor_scalar(tiles[2][:], top[:, 0:E], 1.0 / P, None, ALU.mult))
            chain(dve.tensor_tensor(over[:], bc(tiles[2][:], [P, E, KT], 2), thresholds, ALU.is_gt))
            chain(dve.tensor_reduce(tiles[0][:], over[:], AX.X, ALU.add))
            dve.tensor_copy(tiles[2][:], tiles[0][:])
            src = 0
            for d in (1, 2, 4):
                a, z = tiles[src], tiles[1 - src]
                dve.tensor_copy(z[:, 0:d], a[:, 0:d])
                chain(dve.tensor_tensor(z[:, d:E], a[:, d:E], a[:, 0:E - d], ALU.add))
                src = 1 - src
            ends = tiles[src]
            dve.tensor_tensor(slot_of[:], before[:], ranks, ALU.add)
            chain(dve.tensor_tensor(tiles[2][:], ends[:], tiles[2][:], ALU.subtract))
            chain(dve.scalar_tensor_tensor(slot_of[:], bc(tiles[2][:], full, 1), float(P), slot_of[:], ALU.mult, ALU.add))
            for k, (mask, part) in enumerate(((first, cand), (second, prob2))):
                dve.tensor_tensor(part[:], mask[:], slot_of[:], ALU.mult).then_inc(routed, 1)
                n[0] += 1
            dve.wait_ge(routed, n[0])
            dve.tensor_reduce(slot_f[:, 0, :], cand[:], AX.X, ALU.add)
            chain(dve.tensor_reduce(slot_f[:, 1, :], prob2[:], AX.X, ALU.add))
            chain(dve.tensor_copy(slot_i[:], slot_f[:]))
            chain(dve.tensor_scalar(place_i[:], slot_i[:], P - 1, None, ALU.bitwise_and))
            chain(dve.tensor_copy(place[:], place_i[:]))
            chain(dve.tensor_tensor(tile_of[:], slot_f[:], place[:], ALU.subtract))
            chain(dve.tensor_scalar(tile_of[:], tile_of[:], 1.0 / P, None, ALU.mult))
            by_tile = [P, B, TILES]
            columns = iota_f[:, 0:TILES].rearrange("p (a t) -> p a t", a=1).to_broadcast(by_tile)
            for k in range(2):
                dve.tensor_tensor(tile_hot[:, k], columns, bc(tile_of[:, k, :], by_tile, 2), ALU.is_equal).then_inc(tile_eq_ready, 1)
            for k in range(2):
                for b in range(B):
                    dve.tensor_scalar(place_hot[:, k, b, :], iota_f[:], place[:, k, b:b + 1], None,
                                      ALU.is_equal).then_inc(place_hot_ready, 1)
            chain(dve.tensor_tensor(past[:], ends[0:1, :].rearrange("p (a e) -> p a e", a=1).to_broadcast([1, TILES + 1, E]),
                                    iota_f[0:1, 0:TILES + 1].rearrange("p (t a) -> p t a", a=1).to_broadcast([1, TILES + 1, E]), ALU.is_le))
            chain(dve.tensor_reduce(tile_f[:], past[:], AX.X, ALU.add))
            for at, size in ((w_at, DC * F), (b1_at, FC), (b2_at, D)):
                dve.tensor_scalar(at[:], tile_f[:], float(E - 1), float(size), ALU.min, ALU.mult).then_inc(table_ready, 1)
            dve.wait_ge(pe_b1, 1)
            dve.tensor_copy(b1T[:], h_bank[0][:, 0:E * FC]).then_inc(b1_ready, 1)
            dve.wait_ge(marks_in, 1)
            chain(dve.tensor_copy(slot_mark[:], y_bank[1][:, 0:TILES]))
            dve.tensor_scalar(slot_row[:], slot_mark[:], 0.0, float(B * P), ALU.is_lt, ALU.mult)
            dve.scalar_tensor_tensor(slot_pad[:], slot_mark[:], 0.0, pad_rows[:], ALU.is_equal, ALU.mult)
            chain(dve.scalar_tensor_tensor(slot_token[:], slot_mark[:], -1.0, slot_mark[:], ALU.mult, ALU.max))
            chain(dve.tensor_scalar(slot_token[:], slot_token[:], 1.0, -1.0, ALU.max, ALU.add))
            dve.tensor_copy(token_ids[:], slot_token[:])
            chain(dve.tensor_tensor(slot_row[:], slot_row[:], slot_token[:], ALU.add))
            chain(dve.tensor_tensor(slot_row[:], slot_row[:], slot_pad[:], ALU.add))
            dve.tensor_copy(row_ids[:], slot_row[:]).then_inc(ids_ready, 1)
            dve.wait_ge(loaded, 32)
            dve.wait_ge(table_ready, 3)

            def step(i, par, at):
                def split(t, tp, k):
                    half = slice(k * 512, (k + 1) * 512)
                    dve.wait_ge(act_h, count(t, 2, k + 1))
                    if k == 0 and (not isinstance(t, int) or t >= 2):
                        dve.wait_ge(pe_y, t - 1)
                    dve.tensor_scalar(hh[tp][:, half], h[tp][:, half], XS, None, ALU.mult).then_inc(dve_hi, 1)
                    dve.wait_ge(dve_hi, count(t, 2, k + 1))
                    dve.scalar_tensor_tensor(hl[tp][:, half], h[tp][:, half], XS, hh[tp][:, half],
                                             ALU.mult, ALU.subtract).then_inc(dve_lo, 1)

                if within(i):
                    split(i, par, 1)
                if within(i + 2):
                    t = i + 2
                    dve.wait_ge(pe_x, t + 1)
                    if not isinstance(t, int) or t >= 2:
                        dve.wait_ge(pe_h, count(t - 2, 2))
                    dve.tensor_copy(xgT[par][:], x_bank[:, 0:2 * D].rearrange("p (c t) -> p c t", t=P)).then_inc(dve_x, 1)
                if within(i + 1):
                    split(i + 1, 1 - par, 0)
                if within(i):
                    dve.wait_ge(pe_y, i + 1)
                    if not isinstance(i, int) or i >= 2:
                        dve.wait_ge(y_scattered[par], shared(i - 2, par))
                    dve.scalar_tensor_tensor(y[par][:], y_bank[par][:, 0:D], 1.0 / (XS * WS), b2_bc[:, bass.ds(at[0], D)],
                                             ALU.mult, ALU.add).then_inc(dve_y, 1)

            run_tiles(dve, step, mybir.EngineType.DVE, b2_at, (E - 1) * D)
            for b in range(B):
                q, j = divmod(b, QB)
                xb = x1[:, b * D:(b + 1) * D]
                if j == 0:
                    dve.wait_ge(y_loaded[q % 2], 32 * (q // 2 + 1))
                chain(dve.scalar_tensor_tensor(xb, yq[q % 2][:, 0, j], weight[0][:, b:b + 1], xb, ALU.mult, ALU.add))
                dve.scalar_tensor_tensor(xb, yq[q % 2][:, 1, j], weight[1][:, b:b + 1], xb, ALU.mult, ALU.add).then_inc(combined, 1)

        @block.tensor
        def _(pe):
            pe.wait_ge(loaded, 32)
            pe.transpose(h_bank[0][:, 0:E * FC], b1_rows[:], ident[0:E * FC, 0:E * FC]).then_inc(pe_b1, 1)
            pe.wait_ge(consts, CONSTS)
            pe.wait_ge(ranks_in, 1)
            flat = chosen[:].rearrange("p b e -> p (b e)")
            pe.matmul(r_bank[:, 0:P], below[:], flat, start=True, stop=True)
            pe.matmul(r_bank[:, P:2 * P], ones[:], flat, start=True, stop=True).then_inc(ranks_ready, 1)
            for k in range(2):
                pe.wait_ge(tile_hot_ready, k + 1)
                for b in range(B):
                    pe.wait_ge(place_hot_ready, k * B + b + 1)
                    last = pe.matmul(y_bank[1][:, 0:TILES], place_hot[:, k, b, :], tile_hot[:, k, b, :],
                                     start=(k == 0 and b == 0), stop=(k == 1 and b == B - 1))
            last.then_inc(marks_in, 1)
            pe.wait_ge(ids_ready, 1)
            pe.wait_ge(b1_ready, 1)
            pe.wait_ge(table_ready, 3)

            def step(i, par, at):
                t, tp = i + 1, 1 - par
                if within(t):
                    pe.wait_ge(dve_x, t + 1)
                for f in range(FC):
                    k, c = divmod(f, 4)
                    if within(t):
                        if c == 0 and (not isinstance(t, int) or t >= 2):
                            pe.wait_ge(act_h, count(t - 2, 2, k + 1))
                        terms = [(w, x, d) for d in range(DC) for w, x in ((w1h, 0), (w1h, DC), (w1l, 0))]
                        for m, (w, x, d) in enumerate(terms):
                            last = pe.matmul(h_bank[2 * tp + k][:, c * P:(c + 1) * P],
                                             w[:, bass.ds(at[1] + (d * F + f * P), P)], xgT[tp][:, x + d, :],
                                             start=(m == 0), stop=(m == len(terms) - 1))
                        if c == 3:
                            last.then_inc(pe_h, 1)
                    if f == 3 and within(i + 2):
                        pe.wait_ge(x_gathered[par], shared(i + 2, par))
                        if not isinstance(i, int) or i + 2 >= 1:
                            pe.wait_ge(dve_x, i + 2)
                        for n in range(2 * DC):
                            last = pe.transpose(x_bank[:, n * P:(n + 1) * P], xg[par][:, n * P:(n + 1) * P], ident16[:])
                        last.then_inc(pe_x, 1)
                    if within(i):
                        if f == 0 and (not isinstance(i, int) or i >= 2):
                            pe.wait_ge(dve_y, i - 1)
                        if c == 0:
                            pe.wait_ge(dve_lo, count(i, 2, k + 1))
                        for m, (a, w) in enumerate(((hh, w2h), (hl, w2h), (hh, w2l))):
                            last = pe.matmul(y_bank[par][:, 0:D], a[par][:, f * P:(f + 1) * P],
                                             w[:, bass.ds(at[0] + f * D, D)],
                                             start=(f == 0 and m == 0), stop=(f == FC - 1 and m == 2))
                if within(i):
                    last.then_inc(pe_y, 1)

            run_tiles(pe, step, mybir.EngineType.PE, w_at, (E - 1) * DC * F)


_INS = ['x', 'ctx_1024', 'fside_BxSx2_0', 'L0_xattn_Wq', 'L0_xattn_Wkv', 'L0_xattn_Wout', 'L0_xattn_bout',
        'L0_ffn_gate_w', 'L0_ffn_gate_b', 'L0_ffn_w1', 'L0_ffn_b1', 'L0_ffn_w2', 'L0_ffn_b2']
_OUTS = [((16, 128, 256), 'float32')]


def kernel(**inputs):
    import numpy as _np
    import concourse.bacc as _bacc
    from concourse import mybir as _mybir
    from concourse.bass_utils import run_bass_kernel_spmd as _run

    nc = _bacc.Bacc("TRN2", target_bir_lowering=False, num_devices=1)
    arrays, args = {}, []
    for name in _INS:
        a = _np.ascontiguousarray(inputs[name])
        arrays[f"in_{name}_dram"] = a
        args.append(nc.dram_tensor(f"in_{name}_dram", a.shape, _mybir.dt.from_np(a.dtype), kind="ExternalInput").ap())
    for i, (shape, dtype) in enumerate(_OUTS):
        dt = _mybir.dt.from_np(_np.dtype(dtype))
        args.append(nc.dram_tensor(f"out_{i}_dram", shape, dt, kind="ExternalOutput").ap())
    build(nc, *args)
    r = _run(nc, [arrays], core_ids=[0])
    got = tuple(r.results[0][f"out_{i}_dram"] for i in range(len(_OUTS)))
    return got[0]
```

```python
from contextlib import ExitStack
import math

import numpy as np
import concourse.bass as bass
from concourse import mybir

F32 = mybir.dt.float32
F16 = mybir.dt.float16
I32 = mybir.dt.int32
ALU = mybir.AluOpType
ACT = mybir.ActivationFunctionType
AX = mybir.AxisListType

P = 128
B = 16
D = 256
DC = D // P
CD = 128
H = 32
HD = D // H
SLOT = 32
ROWT = P // SLOT
HG = H // ROWT
UNITS = 8
UH = H // UNITS
VW = SLOT
HALF = UNITS // 2
FIRST = 4
NPB = 2
E = 8
F = 1024
FC = F // P
EPS = 1e-5
QS = 64.0
XS = 64.0
WS = 256.0
MROW = 3 * HD
EXP_SCALE = 1.0 / (QS * QS * math.sqrt(HD))
TWO_PI = 2.0 * math.pi
ROW = D + 2
TILES = 2 * B + E - 1
RSQRT_OPS = 15
CHAIN2 = 11
RSQRT_MAGIC = float(0x5F3759DF)


def count(b, per, k=None):
    return b * per + (per if k is None else k)


def rsqrt(eng, var, y, t, ti, done, base):
    n = [0]

    def chain(ins):
        n[0] += 1
        ins.then_inc(done, 1)
        eng.wait_ge(done, base + n[0])

    chain(eng.tensor_scalar(t[:, 0], var, EPS, None, ALU.add))
    chain(eng.tensor_copy(t[:, 1], t[:, 0].bitcast(I32)))
    chain(eng.tensor_scalar(ti, t[:, 1], -0.5, RSQRT_MAGIC, ALU.mult, ALU.add))
    guess = ti.bitcast(F32)
    for i in range(3):
        y_in = guess if i == 0 else y
        chain(eng.tensor_tensor(t[:, 1], y_in, y_in, ALU.mult))
        chain(eng.tensor_tensor(t[:, 2], t[:, 1], t[:, 0], ALU.mult))
        chain(eng.tensor_scalar(t[:, 2], t[:, 2], -0.5, 1.5, ALU.mult, ALU.add))
        chain(eng.tensor_tensor(y, y_in, t[:, 2], ALU.mult))


def build(nc, x, ctx_in, pos, wq, wkv, wout, bout, gate_w, gate_b, w1, b1, w2, b2, out):
    with ExitStack() as ctx:
        def sb(name, shape, dt):
            return ctx.enter_context(nc.sbuf_tensor(name, shape, dt))

        x1 = sb("x1", [P, B * D], F32)
        logits = sb("logits", [P, B, E], F32)
        w1h = sb("w1h", [P, E * DC * F], F16)
        w1l = sb("w1l", [P, E * DC * F], F16)
        w2h = sb("w2h", [P, E * FC * D], F16)
        w2l = sb("w2l", [P, E * FC * D], F16)
        ident = sb("ident", [P, P], F32)
        ident16 = sb("ident16", [P, P], F16)
        x2 = sb("x2", [P, 2, 2 * D], F16)

        tables = {
            "ones": sb("ones", [P, P], F16),
            "lower": sb("lower", [P, E, E], F16),
            "iota_16": sb("iota_16", [P, P], F16),
            "iota_f": sb("iota_f", [P, TILES + 1], F32),
            "marks": sb("marks", [P, 2, B], F32),
            "tile_first": sb("tile_first", [P, TILES], F32),
            "pad_row": sb("pad_row", [P, 1], F32),
        }

        x2_dram = nc.dram_tensor("x2_dram", (B * P, ROW), I32, kind="Internal").ap()
        sum_dram = nc.dram_tensor("sum_dram", (B * P + P, D), F32, kind="Internal").ap()

        x2_stored = [ctx.enter_context(nc.semaphore(f"x2_stored{i}")) for i in range(2)]
        sum_stored = ctx.enter_context(nc.semaphore("sum_stored"))

        attention(nc, x, ctx_in, pos, wq, wkv, wout, bout, gate_w, gate_b, w1, w2, x1, x2, logits,
                  w1h, w1l, w2h, w2l, ident, ident16, tables, x2_dram, sum_dram, x2_stored, sum_stored)
        experts(nc, b1, b2, out, logits, w1h, w1l, w2h, w2l, ident, ident16, tables,
                x2_dram, sum_dram, x2_stored, sum_stored)


def attention(nc, x, ctx_in, pos, wq, wkv, wout, bout, gate_w, gate_b, w1, w2, x1, x2, logits,
              w1h, w1l, w2h, w2l, ident, ident16, tables, x2_dram, sum_dram, x2_stored, sum_stored):
    w1_chunks = w1.rearrange("e (k p) f -> (e k) p f", p=P)
    w2_chunks = w2.rearrange("e (h c p) d -> (e h) p c d", p=P, h=2)

    with ExitStack() as ctx:
        def sb(name, shape, dt):
            return ctx.enter_context(nc.sbuf_tensor(name, shape, dt))

        def bank(name, shape, dt):
            return ctx.enter_context(nc.psum_tensor(name, shape, dt))

        def sem(name):
            return ctx.enter_context(nc.semaphore(name))

        wq_sb = sb("wq_sb", [P, DC, D], F32)
        wkv_sb = sb("wkv_sb", [P, 2 * D], F32)
        wout_sb = sb("wout_sb", [P, DC, D], F32)
        bout_bc = sb("bout_bc", [P, D], F32)
        gw_sb = sb("gw_sb", [P, DC, E], F32)
        gb_bc = sb("gb_bc", [P, E], F32)
        pos_sb = sb("pos_sb", [P, B, 2], F32)
        cos8 = sb("cos8", [P, B * HD], F32)
        sin8 = sb("sin8", [P, B * HD], F32)
        bn1 = sb("bn1", [P, B * 6], F32)
        mv1 = sb("mv1", [P, B * 2], F32)
        rs1 = sb("rs1", [P, B], F32)
        nt1 = sb("nt1", [P, 3, B], F32)
        nt1i = sb("nt1i", [P, B], I32)
        bn2 = sb("bn2", [P, 6], F32)
        mv2 = sb("mv2", [P, 2], F32)
        rs2 = sb("rs2", [P, 1], F32)
        nt2 = sb("nt2", [P, 3], F32)
        nt2i = sb("nt2i", [P, 1], I32)
        ctx_sb = sb("ctx_sb", [P, 2, CD], F32)
        xhat = sb("xhat", [P, D], F32)
        xT = sb("xT", [P, DC, P], F32)
        ctxT = [sb(f"ctxT{i}", [P, P], F32) for i in range(2)]
        qk = sb("qk", [P, 2, D], F32)
        qks = sb("qks", [P, 2, D], F32)
        qx = [sb(f"qx{i}", [P, H, SLOT], F16) for i in range(2)]
        kx = sb("kx", [P, H, SLOT], F16)
        qT = [sb(f"qT{i}", [P, HG, P], F16) for i in range(2)]
        kT = [sb(f"kT{i}", [P, HG, P], F16) for i in range(2)]
        v = [sb(f"v{i}", [P, H, VW], F32) for i in range(2)]
        mx = sb("mx", [P, H], F32)
        probs = [sb(f"probs{i}", [P, UH * P], F32) for i in range(NPB)]
        recip = sb("recip", [P, HALF * UH], F32)
        o_sb = [sb(f"o_sb{i}", [P, HALF * P], F32) for i in range(2)]
        attn = sb("attn", [P, D], F32)
        turned = sb("turned", [P, DC, P], F32)
        x1b = sb("x1b", [P, D], F32)
        x2f = sb("x2f", [P, D], F32)
        w1_stage = sb("w1_stage", [P, F], F32)
        w2_stage = sb("w2_stage", [P, F], F32)
        ang, turns, turns_i, sincos = [o_sb[0][:, i * P:(i + 1) * P].rearrange("p (k n) -> p k n", k=2) for i in range(4)]
        turns_i = turns_i.bitcast(I32)

        s_bank = [bank(f"s_bank{i}", [P, 512], F32) for i in range(2)]
        t_bank = [bank(f"t_bank{i}", [P, 512], F32) for i in range(2)]
        o_bank = bank("o_bank", [P, HALF * P], F32)
        m0 = bank("m0", [P, 512], F32)
        m1 = bank("m1", [P, 512], F32)
        m2 = bank("m2", [P, 512], F32)
        tq1_16 = m0[:, :].bitcast(F16)
        tk_16 = s_bank[0][:, :].bitcast(F16)
        tq2_16 = s_bank[1][:, :].bitcast(F16)

        names = """consts_ready setup_v setup_a setup_p x_loaded x_rest_loaded pos_loaded small_loaded
        w1_loaded w2_loaded tables_ready slots_ready stats1_ready wholes_ready routing_ready
        pe_xT pe_qk pe_v pe_tk pe_tq1 pe_tq2 pe_s pe_st pe_av pe_oT pe_attnT pe_out pe_x2T pe_gate
        act_xT act_qk act_v act_tk act_x1 act_hi act_exp act_o act_attnT act_x2hi act_x2T act_w
        dve_ws dve_max dve_m dve_tq1 dve_tq2 dve_rec dve_norm dve_x1 dve_bn dve_stats dve_gate
        dve_xhat pool_xb pool_mul pool_rope pool_lo dve_chain dve_x2 pool_x2lo pool_w""".split()
        sems = {n: sem(n) for n in names}
        (consts_ready, setup_v, setup_a, setup_p, x_loaded, x_rest_loaded, pos_loaded, small_loaded,
         w1_loaded, w2_loaded, tables_ready, slots_ready, stats1_ready, wholes_ready, routing_ready,
         pe_xT, pe_qk, pe_v, pe_tk, pe_tq1, pe_tq2, pe_s, pe_st, pe_av, pe_oT, pe_attnT, pe_out, pe_x2T, pe_gate,
         act_xT, act_qk, act_v, act_tk, act_x1, act_hi, act_exp, act_o, act_attnT, act_x2hi, act_x2T, act_w,
         dve_ws, dve_max, dve_m, dve_tq1, dve_tq2, dve_rec, dve_norm, dve_x1, dve_bn, dve_stats, dve_gate,
         dve_xhat, pool_xb, pool_mul, pool_rope, pool_lo, dve_chain, dve_x2, pool_x2lo, pool_w) = [sems[n] for n in names]
        ctx_loaded = [sem(f"ctx_loaded{i}") for i in range(2)]

        def paired(b, par):
            return 8 * b + (16 if par == 0 else 8)

        def run_steps(eng, step):
            for s in range(-2, 4):
                step(s, s % 2)
            with eng.Fori(2, B // 2 - 2) as pair:
                step(2 * pair, 0)
                step(2 * pair + 1, 1)
            for s in range(B - 4, B + 3):
                step(s, s % 2)

        def has(b):
            return not isinstance(b, int) or 0 <= b < B

        def peeled(s):
            return isinstance(s, int)

        block = ctx.enter_context(nc.Block())

        @block.sync
        def _(sp):
            sp.dma_start(pos_sb[:], pos.rearrange("b p c -> p b c")).then_inc(pos_loaded, 16)
            x1_by_batch = x1[:, :].rearrange("p (b d) -> p b d", b=B)
            x_by_batch = x.rearrange("b p d -> p b d")
            sp.dma_start(x1_by_batch[:, 0:FIRST], x_by_batch[:, 0:FIRST]).then_inc(x_loaded, 16)
            for i in range(2):
                sp.dma_start(ctx_sb[:, i, :], ctx_in[i]).then_inc(ctx_loaded[i], 16)
            sp.dma_start(wq_sb[:], wq.rearrange("(c p) n -> p c n", p=P)).then_inc(small_loaded, 16)
            sp.dma_start(wkv_sb[:], wkv).then_inc(small_loaded, 16)
            sp.dma_start(x1_by_batch[:, FIRST:B], x_by_batch[:, FIRST:B]).then_inc(x_rest_loaded, 16)
            wout_heads = wout.rearrange("(a i j d) n -> a j i d n", a=2, i=UH, d=HD)
            for u in range(UNITS):
                sp.dma_start(wout_sb[(u % HALF) * SLOT:(u % HALF + 1) * SLOT, u // HALF, :],
                             wout_heads[u % 2, u // 2]).then_inc(small_loaded, 16)
            sp.dma_start(gw_sb[:], gate_w.rearrange("(c p) n -> p c n", p=P)).then_inc(small_loaded, 16)
            sp.dma_start(bout_bc[:], bout.rearrange("(a d) -> a d", a=1).to_broadcast([P, D])).then_inc(small_loaded, 16)
            sp.dma_start(gb_bc[:], gate_b.rearrange("(a d) -> a d", a=1).to_broadcast([P, E])).then_inc(small_loaded, 16)

            def step(s, par):
                c = s + 4
                if has(c):
                    sp.wait_ge(pe_xT, count(s + 2, 1))
                    sp.dma_start(ctx_sb[:, par, :], ctx_in[c] if peeled(s) else ctx_in[bass.ds(c, 1)].rearrange("a p c -> (a p) c")).then_inc(ctx_loaded[par], 16)
                if has(s + 1):
                    if has(s):
                        sp.wait_ge(act_w, count(s, 2, 1))
                        sp.wait_ge(pool_w, count(s, 2, 1))
                    c = s + 1
                    one = w1_chunks[c] if peeled(s) else w1_chunks[bass.ds(c, 1)].rearrange("a p f -> (a p) f")
                    two = w2_chunks[c] if peeled(s) else w2_chunks[bass.ds(c, 1)].rearrange("a p c d -> (a p) c d")
                    sp.dma_start(w1_stage[:], one).then_inc(w1_loaded, 16)
                    if has(s):
                        sp.wait_ge(act_w, count(s, 2))
                        sp.wait_ge(pool_w, count(s, 2))
                    sp.dma_start(w2_stage[:].rearrange("p (c d) -> p c d", d=D), two).then_inc(w2_loaded, 16)

                b = s - 2
                if has(b):
                    sp.wait_ge(pool_x2lo, count(b, 1))
                    sp.dma_start(x2_dram[bass.ds(b * P, P), 0:D], x2[:, par, :].bitcast(I32)).then_inc(x2_stored[par], 16)
                    sp.wait_ge(act_x1, count(b, 1))
                    sp.dma_start(sum_dram[bass.ds(b * P, P), :], x1[:, bass.ds(b * D, D)]).then_inc(sum_stored, 16)

            run_steps(sp, step)
            sp.dma_start(sum_dram[B * P:(B + 1) * P, :], x1[:, 0:D]).then_inc(sum_stored, 16)

        @block.gpsimd
        def _(pool):
            pool.memset(ident[:], 0.0).then_inc(setup_p, 1)
            pool.wait_ge(setup_p, 1)
            pool.affine_select(out=ident[:], in_=ident[:], compare_op=ALU.not_equal, fill=1.0, base=0,
                               pattern=[[-1, P]], channel_multiplier=1).then_inc(setup_p, 1)
            pool.wait_ge(setup_p, 2)
            pool.tensor_copy(ident16[:], ident[:]).then_inc(consts_ready, 1)
            pool.memset(qx[0][:], 0.0)
            pool.memset(qx[1][:], 0.0)
            pool.memset(kx[:], 0.0).then_inc(setup_p, 1)
            pool.memset(v[0][:], 1.0)
            pool.memset(v[1][:], 1.0)
            pool.wait_ge(setup_p, 3)
            pool.memset(kx[:, :, MROW], QS).then_inc(slots_ready, 1)

            ones, lower, marks = (tables[k] for k in ("ones", "lower", "marks"))
            whole = probs[0][:].bitcast(I32)
            iota_i = whole[:, 0:P]
            mark_i = whole[:, P:P + B]
            pad_i = whole[:, P + B:P + B + 1]
            tile_first_i = whole[:, P + B + 1:P + B + 1 + TILES]
            pool.memset(ones[:], 1.0).then_inc(wholes_ready, 1)
            pool.memset(lower[:], 1.0).then_inc(wholes_ready, 1)
            pool.iota(iota_i, pattern=[[1, P]], base=0, channel_multiplier=0).then_inc(wholes_ready, 1)
            pool.iota(mark_i, pattern=[[P, B]], base=1, channel_multiplier=1).then_inc(wholes_ready, 1)
            pool.iota(pad_i, pattern=[[0, 1]], base=B * P, channel_multiplier=1).then_inc(wholes_ready, 1)
            pool.iota(tile_first_i, pattern=[[P, TILES]], base=0, channel_multiplier=0).then_inc(wholes_ready, 1)
            pool.wait_ge(wholes_ready, 6)
            pool.affine_select(out=lower[:], in_=lower[:], compare_op=ALU.is_gt, fill=0.0, base=0,
                               pattern=[[1, E], [-1, E]], channel_multiplier=0)
            pool.tensor_copy(tables["iota_f"][:], iota_i[:, 0:TILES + 1])
            pool.tensor_copy(tables["iota_16"][:], iota_i)
            pool.tensor_copy(tables["pad_row"][:], pad_i)
            pool.tensor_copy(tables["tile_first"][:], tile_first_i)
            pool.tensor_copy(marks[:, 0, :], mark_i).then_inc(routing_ready, 1)
            pool.wait_ge(routing_ready, 1)
            pool.tensor_scalar(marks[:, 1, :], marks[:, 0, :], -1.0, None, ALU.mult)

            def alone():
                pool.wait_ge(consts_ready, 1)

            def add_bias(b):
                pool.wait_ge(dve_xhat, count(b, 1))
                alone()
                xb = x1[:, bass.ds(b * D, D)]
                pool.tensor_tensor(xb, xb, bout_bc[:], ALU.add).then_inc(pool_xb, 1)

            def step(s, par):
                b = s + 1
                if has(b):
                    pool.wait_ge(act_hi, count(b, 1))
                    q4 = qx[1 - par][:].rearrange("p h (k d) -> p h k d", d=HD)
                    k4 = kx[:].rearrange("p h (k d) -> p h k d", d=HD)
                    pool.tensor_tensor(q4[:, :, 2, :], qk[:, 0, :].rearrange("p (h d) -> p h d", d=HD), q4[:, :, 0, :],
                                       ALU.subtract)
                    pool.tensor_tensor(k4[:, :, 1, :], qk[:, 1, :].rearrange("p (h d) -> p h d", d=HD), k4[:, :, 0, :],
                                       ALU.subtract).then_inc(pool_lo, 1)
                if has(s):
                    pool.wait_ge(act_w, count(s, 2, 1))
                    alone()
                    pool.tensor_tensor(w1l[:, bass.ds(s * F, F)], w1_stage[:], w1h[:, bass.ds(s * F, F)],
                                       ALU.subtract).then_inc(pool_w, 1)
                    pool.wait_ge(act_w, count(s, 2))
                    alone()
                    pool.tensor_tensor(w2l[:, bass.ds(s * F, F)], w2_stage[:], w2h[:, bass.ds(s * F, F)],
                                       ALU.subtract).then_inc(pool_w, 1)
                b = s + 2
                if has(b):
                    pool.wait_ge(act_qk, count(b, 1))
                    if peeled(b) and b == 0:
                        pool.wait_ge(tables_ready, 1)
                    for i, (dst, table) in enumerate(((qks, sin8), (qk, cos8))):
                        for j in range(2):
                            tab = table[:, bass.ds(b * HD, HD)].rearrange("p (a d) -> p a d", a=1).to_broadcast([P, H, HD])
                            pool.tensor_tensor(dst[:, j, :].rearrange("p (h d) -> p h d", d=HD),
                                               qk[:, j, :].rearrange("p (h d) -> p h d", d=HD), tab, ALU.mult).then_inc(pool_mul, 1)
                    pool.wait_ge(pool_mul, count(b, 4))
                    pairs_c = qk[:].rearrange("p i (n e) -> p (i n) e", e=2)
                    pairs_s = qks[:].rearrange("p i (n e) -> p (i n) e", e=2)
                    pool.tensor_tensor(pairs_c[:, :, 0], pairs_c[:, :, 0], pairs_s[:, :, 1], ALU.add)
                    pool.tensor_tensor(pairs_c[:, :, 1], pairs_c[:, :, 1], pairs_s[:, :, 0], ALU.add).then_inc(pool_rope, 1)
                b = s - 2
                if has(b):
                    pool.wait_ge(act_x2hi, count(b, 1))
                    pool.tensor_tensor(x2[:, par, D:2 * D], x2f[:], x2[:, par, 0:D],
                                       ALU.subtract).then_inc(pool_x2lo, 1)
                if has(s + 2):
                    add_bias(s + 2)

            pool.wait_ge(small_loaded, 16 * (5 + UNITS))
            run_steps(pool, step)

        @block.scalar
        def _(act):
            act.wait_ge(setup_v, 11)
            act.activation(sincos[:], ang[:], ACT.Sin).then_inc(setup_a, 1)

            def exp_unit(b, u):
                act.wait_ge(pe_st, count(b, UNITS, u + 1))
                act.activation(probs[u % NPB][:], t_bank[u % 2][:], ACT.Exp, scale=EXP_SCALE).then_inc(act_exp, 1)

            def split_weights(s, k):
                stage, hi, ready = ((w1_stage, w1h, 1), (w2_stage, w2h, 2))[k]
                act.wait_ge(dve_ws, count(s, 2, ready))
                act.copy(hi[:, bass.ds(s * F, F)], stage[:]).then_inc(act_w, 1)

            def step(s, par):
                def values(k):
                    act.wait_ge(pe_av, count(s - 1, UNITS, (k + 1) * HALF))
                    act.copy(o_sb[k][:], o_bank[:]).then_inc(act_o, 1)

                for u in range(UNITS):
                    if has(s - 1):
                        exp_unit(s - 1, u)
                    if u == HALF and has(s - 1):
                        values(0)
                    if u == 0 and has(s - 3):
                        b = s - 3
                        act.wait_ge(pe_x2T, count(b, 1))
                        act.mul(turned[:], m0[:, 0:D].rearrange("p (c t) -> p c t", c=DC), 1.0 / XS).then_inc(act_x2T, 1)
                    if u == 1 and has(s - 2):
                        b = s - 2
                        act.wait_ge(pe_attnT, count(b, 1))
                        if has(b - 1):
                            act.wait_ge(pe_gate, count(b - 1, 1))
                        act.copy(turned[:], m2[:, 0:D].rearrange("p (c t) -> p c t", c=DC)).then_inc(act_attnT, 1)
                    if u == 1 and has(s):
                        act.wait_ge(pe_v, count(s, 1))
                        if peeled(s) and s == 0:
                            act.wait_ge(slots_ready, 1)
                        act.copy(v[par][:, :, 0:HD], m1[:, 0:D].rearrange("p (h d) -> p h d", d=HD)).then_inc(act_v, 1)
                    if u == 2 and has(s + 1):
                        b = s + 1
                        act.wait_ge(pool_rope, count(b, 1))
                        if peeled(b) and b == 0:
                            act.wait_ge(slots_ready, 1)
                        q4 = qx[1 - par][:].rearrange("p h (k d) -> p h k d", d=HD)
                        k4 = kx[:].rearrange("p h (k d) -> p h k d", d=HD)
                        qr = qk[:, 0, :].rearrange("p (h a d) -> p h a d", a=1, d=HD).to_broadcast([P, H, 2, HD])
                        kr = qk[:, 1, :].rearrange("p (h a d) -> p h a d", a=1, d=HD).to_broadcast([P, H, 2, HD])
                        act.copy(q4[:, :, 0:2, :], qr)
                        act.copy(k4[:, :, 0:4:2, :], kr).then_inc(act_hi, 1)
                    if u == 3 and has(s + 2):
                        b = s + 2
                        act.wait_ge(pe_xT, count(b, 1))
                        act.copy(xT[:], m0[:, 0:D].rearrange("p (c t) -> p c t", c=DC))
                        act.copy(ctxT[par][:], m0[:, D:D + P]).then_inc(act_xT, 1)
                    if u in (3, 5) and has(s):
                        split_weights(s, (u - 3) // 2)
                    if u == 4 and has(s - 2):
                        b = s - 2
                        act.wait_ge(dve_x1, count(b, 1))
                        act.copy(x1[:, bass.ds(b * D, D)], x1b[:]).then_inc(act_x1, 1)
                    if u == 6 and has(s + 2):
                        b = s + 2
                        act.wait_ge(pe_qk, count(b, 1))
                        if not peeled(b) or b >= 1:
                            act.wait_ge(pool_lo, count(b - 1, 1))
                        act.copy(qk[:], m1[:].rearrange("p (i d) -> p i d", i=2)).then_inc(act_qk, 1)
                    if u == 7 and has(s - 2):
                        b = s - 2
                        act.wait_ge(dve_x2, count(b, 1))
                        if not peeled(b) or b >= 2:
                            act.wait_ge(x2_stored[par], paired(b - 2, par))
                        act.copy(x2[:, par, 0:D], x2f[:]).then_inc(act_x2hi, 1)
                if has(s + 1):
                    b = s + 1
                    act.wait_ge(pe_tk, count(b, 1))
                    act.copy(kT[1 - par][:], tk_16.rearrange("p (g t) -> p g t", g=HG)).then_inc(act_tk, 1)
                if has(s - 1):
                    values(1)

            run_steps(act, step)

        @block.vector
        def _(dve):
            n = [0]

            def chain(ins):
                n[0] += 1
                ins.then_inc(setup_v, 1)
                dve.wait_ge(setup_v, n[0])

            dve.wait_ge(pos_loaded, 16)
            a4 = ang[:, 0, :].rearrange("p (n j) -> p n j", j=2)
            flat = pos_sb[:].rearrange("p b c -> p (b c)")
            for j in range(2):
                chain(dve.tensor_scalar(a4[:, :, j], flat, float(np.float32(10000.0 ** (-j / 2))), None, ALU.mult))
            chain(dve.tensor_scalar(ang[:, 1, :], ang[:, 0, :], math.pi / 2, None, ALU.add))
            chain(dve.tensor_scalar(turns_i[:], ang[:], 1.0 / TWO_PI, None, ALU.mult))
            chain(dve.tensor_copy(turns[:], turns_i[:]))
            chain(dve.scalar_tensor_tensor(ang[:], turns[:], -TWO_PI, ang[:], ALU.mult, ALU.add))
            for sign, cmp in ((-1.0, ALU.is_gt), (1.0, ALU.is_lt)):
                chain(dve.tensor_scalar(turns[:], ang[:], -sign * math.pi, sign * TWO_PI, cmp, ALU.mult))
                chain(dve.tensor_tensor(ang[:], ang[:], turns[:], ALU.add))
            chain(dve.tensor_scalar(ang[:], ang[:], math.pi, -math.pi, ALU.min, ALU.max))
            def statistics(lo, hi):
                for b in range(lo, hi):
                    n[0] += 1
                    dve.bn_stats(bn1[:, b * 6:(b + 1) * 6], x1[:, b * D:(b + 1) * D]).then_inc(setup_v, 1)
                for b in range(lo, hi):
                    dve.wait_ge(setup_v, n[0] - (hi - 1 - b))
                    dve.bn_aggr(mv1[:, b * 2:b * 2 + 2], bn1[:, b * 6:(b + 1) * 6]).then_inc(stats1_ready, 1)
                dve.wait_ge(stats1_ready, hi)
                var = mv1[:].rearrange("p (b k) -> p b k", k=2)[:, lo:hi, 1]
                rsqrt(dve, var, rs1[:, lo:hi], nt1[:, :, lo:hi], nt1i[:, lo:hi], setup_v, n[0])
                n[0] += RSQRT_OPS

            dve.wait_ge(x_loaded, 16)
            statistics(0, FIRST)
            dve.wait_ge(setup_a, 1)
            c2 = cos8[:].rearrange("p (n e) -> p n e", e=2)
            s2 = sin8[:].rearrange("p (n e) -> p n e", e=2)
            dve.tensor_scalar(c2[:, :, 0], sincos[:, 1, :], QS, None, ALU.mult)
            dve.tensor_scalar(c2[:, :, 1], sincos[:, 1, :], QS, None, ALU.mult)
            dve.tensor_scalar(s2[:, :, 0], sincos[:, 0, :], QS, None, ALU.mult)
            dve.tensor_scalar(s2[:, :, 1], sincos[:, 0, :], -QS, None, ALU.mult).then_inc(tables_ready, 1)

            def normalize(b):
                dve.tensor_scalar(xhat[:], x1[:, bass.ds(b * D, D)], mv1[:, bass.ds(b * 2, 1)], rs1[:, bass.ds(b, 1)],
                                  ALU.subtract, ALU.mult).then_inc(dve_xhat, 1)

            def refine(b, k, y):
                var, a, p = nt2[:, 0:1], nt2[:, 1:2], nt2[:, 2:3]
                steps = ((a, var, y, y, ALU.mult, ALU.mult), (p, a, 3.0 / 8, -10.0 / 8, ALU.mult, ALU.add),
                         (p, p, a, 15.0 / 8, ALU.mult, ALU.add), (rs2[:], p, y, (1.0, XS)[k], ALU.mult, ALU.mult))
                for i, args in enumerate(steps):
                    dve.tensor_scalar(*args).then_inc(dve_chain, 1)
                    dve.wait_ge(dve_chain, count(b, CHAIN2, 3 + 4 * k + i + 1))

            def first_guess(b):
                dve.tensor_scalar(nt2[:, 0:1], mv2[:, 1:2], EPS, None, ALU.add).then_inc(dve_chain, 1)
                dve.wait_ge(dve_chain, count(b, CHAIN2, 1))
                dve.tensor_copy(nt2[:, 1:2], nt2[:, 0:1].bitcast(I32)).then_inc(dve_chain, 1)
                dve.wait_ge(dve_chain, count(b, CHAIN2, 2))
                dve.tensor_scalar(nt2i[:], nt2[:, 1:2], -0.5, RSQRT_MAGIC, ALU.mult, ALU.add).then_inc(dve_chain, 1)
                dve.wait_ge(dve_chain, count(b, CHAIN2, 3))

            mx_units = mx[:].rearrange("p (k g j) -> p k g j", k=2, j=ROWT)

            def divide(b, k):
                oT = m2[:].rearrange("p (n c) -> p n c", c=VW)
                dve.wait_ge(pe_oT, count(b, 2, k + 1))
                dve.reciprocal(recip[:], oT[:, :, HD]).then_inc(dve_rec, 1)
                dve.wait_ge(dve_rec, count(b, 2, k + 1))
                if k == 0 and (not peeled(b) or b >= 1):
                    dve.wait_ge(pe_attnT, count(b - 1, 1))
                dve.tensor_tensor(attn[:, k * P:(k + 1) * P].rearrange("p (n d) -> p n d", d=HD), oT[:, :, 0:HD],
                                  recip[:].rearrange("p (n a) -> p n a", a=1).to_broadcast([P, HALF * UH, HD]),
                                  ALU.mult).then_inc(dve_norm, 1)

            def step(s, par):
                for u in range(UNITS):
                    if u == 4 and has(s - 2):
                        dve.wait_ge(dve_bn, count(s - 2, 1))
                    if has(s):
                        dve.wait_ge(pe_s, count(s, UNITS, u + 1))
                        if u == 0 and (not peeled(s) or s >= 1):
                            dve.wait_ge(dve_m, count(s - 1, 1))
                        dve.tensor_reduce(mx_units[:, u % 2, :, u // 2],
                                          s_bank[u % 2][:].rearrange("p (h k) -> p h k", k=P),
                                          AX.X, ALU.max).then_inc(dve_max, 1)
                    if u == 2 and has(s - 3):
                        b = s - 3
                        dve.wait_ge(pe_gate, count(b, 1))
                        dve.tensor_tensor(logits[:, bass.ds(b, 1), :].rearrange("p a e -> p (a e)"), m0[:, D:D + E], gb_bc[:], ALU.add).then_inc(dve_gate, 1)
                    if u == 3 and has(s - 2):
                        b = s - 2
                        dve.wait_ge(pe_out, count(b, 1))
                        dve.wait_ge(pool_xb, count(b, 1))
                        if not peeled(b) or b >= 1:
                            dve.wait_ge(act_x1, count(b - 1, 1))
                        dve.tensor_tensor(x1b[:], m2[:, D:2 * D], x1[:, bass.ds(b * D, D)], ALU.add).then_inc(dve_x1, 1)
                        dve.wait_ge(dve_x1, count(b, 1))
                        dve.bn_stats(bn2[:], x1b[:]).then_inc(dve_bn, 1)
                    if u == 4 and has(s - 2):
                        dve.bn_aggr(mv2[:], bn2[:]).then_inc(dve_stats, 1)
                    if u == 5 and has(s - 2):
                        dve.wait_ge(dve_stats, count(s - 2, 1))
                        first_guess(s - 2)
                        refine(s - 2, 0, nt2i[:].bitcast(F32))
                    if u == 6 and has(s - 2):
                        b = s - 2
                        refine(b, 1, rs2[:])
                        if not peeled(b) or b >= 1:
                            dve.wait_ge(pe_x2T, count(b - 1, 1))
                            dve.wait_ge(pool_x2lo, count(b - 1, 1))
                        dve.tensor_scalar(x2f[:], x1b[:], mv2[:, 0:1], rs2[:],
                                          ALU.subtract, ALU.mult).then_inc(dve_x2, 1)
                    if u == 0 and has(s - 2):
                        divide(s - 2, 1)
                    if u == 1 and has(s + 2):
                        if has(s + 1):
                            dve.wait_ge(pe_xT, count(s + 1, 1))
                        normalize(s + 2)
                    if u == 1 and peeled(s) and s == -1:
                        dve.wait_ge(x_rest_loaded, 16)
                        statistics(FIRST, B)
                    if u in (1, 3) and has(s):
                        stage, loaded = ((w1_stage, w1_loaded), (w2_stage, w2_loaded))[u // 2]
                        dve.wait_ge(loaded, count(s, 16))
                        dve.tensor_scalar(stage[:], stage[:], WS, None, ALU.mult).then_inc(dve_ws, 1)
                if has(s):
                    dve.wait_ge(dve_max, count(s, UNITS))
                    dve.tensor_scalar(qx[par][:, :, MROW], mx[:], -1.0 / QS, None, ALU.mult).then_inc(dve_m, 1)
                if has(s - 1):
                    divide(s - 1, 0)
                if has(s + 1):
                    dve.wait_ge(pe_tq1, count(s + 1, 1))
                    if has(s - 1):
                        dve.wait_ge(pe_st, count(s - 1, UNITS))
                    dve.tensor_copy(qT[1 - par][:], tq1_16.rearrange("p (g t) -> p g t", g=HG)).then_inc(dve_tq1, 1)
                if has(s):
                    dve.wait_ge(pe_tq2, count(s, 1))
                    dve.tensor_copy(qT[par][:], tq2_16.rearrange("p (g t) -> p g t", g=HG)).then_inc(dve_tq2, 1)

            run_steps(dve, step)

        @block.tensor
        def _(pe):
            pe.wait_ge(consts_ready, 1)
            pe.wait_ge(small_loaded, 16 * (5 + UNITS))

            def pack_T(dst, src, done):
                for g in range(HG):
                    last = pe.transpose(dst[:, g * P:(g + 1) * P],
                                        src[:, g * ROWT:(g + 1) * ROWT, :].rearrange("p h d -> p (h d)"), ident16[:])
                last.then_inc(done, 1)

            def av(b, par, u):
                pe.wait_ge(act_exp, count(b, UNITS, u + 1))
                if u == 0:
                    pe.wait_ge(act_v, count(b, 1))
                if u % HALF == 0:
                    k = u // HALF
                    if k == 1:
                        pe.wait_ge(act_o, count(b, 2, 1))
                for i in range(UH):
                    h = ((u % 2) * UH + i) * ROWT + u // 2
                    last = pe.matmul(o_bank[SLOT * i:SLOT * (i + 1), (u % HALF) * P:(u % HALF + 1) * P],
                                     v[par][:, h, :], probs[u % NPB][:, i * P:(i + 1) * P], start=True, stop=True)
                last.then_inc(pe_av, 1)

            def turn_values(b, k):
                pe.wait_ge(act_o, count(b, 2, k + 1))
                for n in range(HALF):
                    last = pe.transpose(m2[:, n * P:(n + 1) * P], o_sb[k][:, n * P:(n + 1) * P], ident[:])
                last.then_inc(pe_oT, 1)

            def scores(out_bank, stat, mov, rows, u, done):
                j = u // 2
                for i in range(UH):
                    g = (u % 2) * UH + i
                    last = pe.matmul(out_bank[:, i * P:(i + 1) * P], stat[SLOT * j:SLOT * j + rows, g, :],
                                     mov[SLOT * j:SLOT * j + rows, g, :], start=True, stop=True)
                last.then_inc(done, 1)

            def score_unit(s, par, u):
                if u == 0:
                    pe.wait_ge(dve_tq1, count(s, 1))
                    pe.wait_ge(act_tk, count(s, 1))
                if not peeled(s) or s * UNITS + u >= 2:
                    pe.wait_ge(dve_max, count(s, UNITS, u - 1))
                scores(s_bank[u % 2], qT[par], kT[par], MROW, u, pe_s)

            def step(s, par):
                if has(s):
                    score_unit(s, par, 0)
                if has(s - 2):
                    pe.wait_ge(dve_norm, count(s - 2, 2, 1))
                    turn_values(s - 2, 1)
                for u in range(UNITS):
                    if u < UNITS - 1 and has(s):
                        if u == 0 and has(s - 1):
                            pe.wait_ge(dve_tq2, count(s - 1, 1))
                        score_unit(s, par, u + 1)
                    if has(s - 1):
                        b = s - 1
                        if u == 0 and not has(s):
                            pe.wait_ge(dve_tq2, count(b, 1))
                        scores(t_bank[u % 2], kT[1 - par], qT[1 - par], SLOT, u, pe_st)
                    if u == UNITS - 1 and has(s + 1):
                        pe.wait_ge(pool_lo, count(s + 1, 1))
                        if has(s):
                            pe.wait_ge(dve_max, count(s, UNITS, UNITS - 1))
                        pack_T(tk_16, kx, pe_tk)
                    if has(s - 1) and u >= 1:
                        av(s - 1, 1 - par, u - 1)
                    if u == 0 and has(s - 3):
                        b = s - 3
                        pe.wait_ge(dve_x2, count(b, 1))
                        if not has(s):
                            pe.wait_ge(dve_gate, count(b - 1, 1))
                        for c in range(DC):
                            last = pe.transpose(m0[:, c * P:(c + 1) * P], x2f[:, c * P:(c + 1) * P], ident[:])
                        last.then_inc(pe_x2T, 1)
                    if u == 1 and has(s - 2):
                        pe.wait_ge(dve_norm, count(s - 2, 2))
                        for c in range(DC):
                            last = pe.transpose(m2[:, c * P:(c + 1) * P], attn[:, c * P:(c + 1) * P], ident[:])
                        last.then_inc(pe_attnT, 1)
                    if u == 1 and has(s - 3):
                        pe.wait_ge(act_x2T, count(s - 3, 1))
                        for c in range(DC):
                            last = pe.matmul(m0[:, D:D + E], turned[:, c, :], gw_sb[:, c, :], start=(c == 0), stop=(c == DC - 1))
                        last.then_inc(pe_gate, 1)
                    if u == 2 and has(s - 2):
                        pe.wait_ge(act_attnT, count(s - 2, 1))
                        for c in range(DC):
                            last = pe.matmul(m2[:, D:2 * D], turned[:, c, :], wout_sb[:, c, :], start=(c == 0), stop=(c == DC - 1))
                        last.then_inc(pe_out, 1)
                    if u == 3 and has(s + 2):
                        b = s + 2
                        pe.wait_ge(dve_xhat, count(b, 1))
                        pe.wait_ge(ctx_loaded[par], paired(b, par))
                        if has(s - 3):
                            pe.wait_ge(dve_gate, count(s - 3, 1))
                        elif has(s):
                            pe.wait_ge(dve_tq1, count(s, 1))
                        elif has(s + 1):
                            pe.wait_ge(act_xT, count(s + 1, 1))
                        for c in range(DC):
                            pe.transpose(m0[:, c * P:(c + 1) * P], xhat[:, c * P:(c + 1) * P], ident[:])
                        pe.transpose(m0[:, DC * P:(DC + 1) * P], ctx_sb[:, par, :], ident[:]).then_inc(pe_xT, 1)
                    if u == 4 and has(s + 2):
                        pe.wait_ge(act_xT, count(s + 2, 1))
                        if has(s):
                            pe.wait_ge(act_v, count(s, 1))
                        elif has(s + 1):
                            pe.wait_ge(act_qk, count(s + 1, 1))
                        for c in range(DC):
                            pe.matmul(m1[:, 0:D], xT[:, c, :], wq_sb[:, c, :], start=(c == 0), stop=(c == DC - 1))
                    if u == 5 and has(s + 2):
                        pe.matmul(m1[:, D:2 * D], ctxT[par][:], wkv_sb[:, 0:D], start=True, stop=True).then_inc(pe_qk, 1)
                    if u == 6 and has(s - 1):
                        if has(s - 2):
                            pe.wait_ge(dve_x1, count(s - 2, 1))
                        turn_values(s - 1, 0)
                    if u == UNITS - 1 and has(s + 1):
                        if has(s + 2):
                            pe.wait_ge(act_qk, count(s + 2, 1))
                        else:
                            pe.wait_ge(act_v, count(s, 1))
                        pe.matmul(m1[:, 0:D], ctxT[1 - par][:], wkv_sb[:, D:2 * D], start=True, stop=True).then_inc(pe_v, 1)
                        if not has(s + 2):
                            pe.wait_ge(dve_gate, count(s - 3, 1))
                        pack_T(tq1_16, qx[1 - par], pe_tq1)
                if has(s - 1):
                    av(s - 1, 1 - par, UNITS - 1)
                if has(s):
                    pe.wait_ge(dve_m, count(s, 1))
                    pack_T(tq2_16, qx[par], pe_tq2)

            run_steps(pe, step)


def experts(nc, b1, b2, out, logits, w1h, w1l, w2h, w2l, ident, ident16, tables,
            x2_dram, sum_dram, x2_stored, sum_stored):
    with ExitStack() as ctx:
        def sb(name, shape, dt):
            return ctx.enter_context(nc.sbuf_tensor(name, shape, dt))

        def bank(name, shape, dt):
            return ctx.enter_context(nc.psum_tensor(name, shape, dt))

        def sem(name):
            return ctx.enter_context(nc.semaphore(name))

        LAP = 12
        KT = 16
        below = sb("below", [P, P], F16)
        ones, lower, iota_16, iota_f, marks, tile_first, pad_row = (tables[k] for k in (
            "ones", "lower", "iota_16", "iota_f", "marks", "tile_first", "pad_row"))
        b1_rows = sb("b1_rows", [E * FC, P], F32)
        b1T = sb("b1T", [P, E * FC], F32)
        b2_bc = sb("b2_bc", [P, E * D], F32)
        prob = sb("prob", [P, B, E], F32)
        prob2 = sb("prob2", [P, B, E], F32)
        cand = sb("cand", [P, B, E], F32)
        first = sb("first", [P, B, E], F32)
        second = sb("second", [P, B, E], F32)
        chosen = sb("chosen", [P, B, E], F16)
        slot_of = sb("slot_of", [P, B, E], F32)
        top = sb("top", [P, B], F32)
        top1 = sb("top1", [P, B], F32)
        top2 = sb("top2", [P, B], F32)
        norm = sb("norm", [P, B], F32)
        weights = sb("weights", [P, B, 2], F32)
        slot_f = sb("slot_f", [P, 2, B], F32)
        slot_i = sb("slot_i", [P, 2, B], I32)
        place_i = sb("place_i", [P, 2, B], I32)
        place = sb("place", [P, 2, B], F32)
        tile_start = sb("tile_start", [P, 2, B], F32)
        tile_hot = sb("tile_hot", [P, 2, B, TILES], F16)
        place_hot = sb("place_hot", [P, 2, B, P], F16)
        over = sb("over", [P, E, KT], F32)
        load = sb("load", [P, E], F32)
        tiles = sb("tiles", [P, E], F32)
        earlier = sb("earlier", [P, E, E], F32)
        starts = sb("starts", [P, E], F32)
        ends = sb("ends", [P, E], F32)
        past = sb("past", [1, TILES + 1, E], F32)
        tile_f = sb("tile_f", [1, TILES + 1], F32)
        w_at = sb("w_at", [1, TILES + 1], I32)
        b1_at = sb("b1_at", [1, TILES + 1], I32)
        b2_at = sb("b2_at", [1, TILES + 1], I32)
        slot_mark = sb("slot_mark", [P, TILES], F32)
        slot_token = sb("slot_token", [P, TILES], F32)
        slot_row = sb("slot_row", [P, TILES], F32)
        slot_pad = sb("slot_pad", [P, TILES], F32)
        is_choice = [sb(f"is_choice{i}", [P, TILES], F32) for i in range(2)]
        slot_weight = sb("slot_weight", [P, TILES], F32)
        token_ids = sb("token_ids", [P, TILES], I32)
        row_ids = sb("row_ids", [P, TILES], I32)
        spare = sb("spare", [P, 1], F32)
        spare_act = sb("spare_act", [P, 1], F32)
        tile_tokens = [sb(f"tile_tokens{i}", [P, 1], I32) for i in range(2)]
        tile_rows = [sb(f"tile_rows{i}", [P, 1], I32) for i in range(2)]
        xg = [sb(f"xg{i}", [P, ROW], I32) for i in range(2)]
        xgT = [sb(f"xgT{i}", [P, 2 * DC, P], F16) for i in range(2)]
        h = [sb(f"h{i}", [P, FC * P], F32) for i in range(2)]
        hh = [sb(f"hh{i}", [P, FC * P], F16) for i in range(2)]
        hl = [sb(f"hl{i}", [P, FC * P], F16) for i in range(2)]
        y = [sb(f"y{i}", [P, D], F32) for i in range(2)]

        h_bank = [bank(f"h_bank{i}", [P, 512], F32) for i in range(4)]
        x_bank = bank("x_bank", [P, 1024], F16)
        y_bank = [bank(f"y_bank{i}", [P, 512], F32) for i in range(2)]
        r_bank = bank("r_bank", [P, 512], F32)

        names = """below_ready ranks_in loaded shifted exp_ready routed ranks_ready tile_eq_ready b1_ready
        tile_hot_ready place_hot_ready marks_in ids_ready pe_b1 table_ready pool_tokens pool_rows
        pe_x pe_h pe_y dve_x dve_weight dve_hi dve_lo dve_yb dve_y act_h weights_ready weights_stored stored""".split()
        sems = {n: sem("e_" + n) for n in names}
        (below_ready, ranks_in, loaded, shifted, exp_ready, routed, ranks_ready, tile_eq_ready, b1_ready,
         tile_hot_ready, place_hot_ready, marks_in, ids_ready, pe_b1, table_ready, pool_tokens, pool_rows,
         pe_x, pe_h, pe_y, dve_x, dve_weight, dve_hi, dve_lo, dve_yb, dve_y, act_h, weights_ready, weights_stored, stored) = [sems[n] for n in names]
        x_gathered = [sem(f"x_gathered{i}") for i in range(2)]
        y_scattered = [sem(f"y_scattered{i}") for i in range(2)]

        def shared(i, par):
            return 8 * i + (16 if par == 0 else 8)

        def within(i):
            return not isinstance(i, int) or 0 <= i < TILES

        def run_tiles(eng, step, engine=None, table=None, most=0):
            def numbers(i, n):
                if table is None:
                    return [None] * n
                _, values = nc.values_load_multi_w_load_instructions(
                    table[0:1, bass.ds(i, n)], engines=[engine], min_val=0, max_val=most,
                    skip_runtime_bounds_check_because="the tables hold a count of experts, from 0 and cut at E-1, times a size")
                return list(values)

            at = [None] * 3 + numbers(0, LAP + 1)
            for i in range(-3, LAP):
                step(i, i % 2, at[i + 3:i + 5])
            with eng.Fori(1, (TILES - 3) // LAP) as lap:
                at = numbers(LAP * lap, LAP + 1)
                for i in range(LAP):
                    step(LAP * lap + i, i % 2, at[i:i + 2])
            at = numbers(TILES - 3, 4)
            for i in range(3):
                step(TILES - 3 + i, (TILES - 3 + i) % 2, at[i:i + 2])

        def bc(ap, shape, at):
            s = {1: "p (a n) -> p a n", 2: "p (n a) -> p n a"}[at]
            return ap.rearrange(s, a=1).to_broadcast(shape)

        PARTS = 4
        out_rows = out.rearrange("b p d -> (b p) d")
        block = ctx.enter_context(nc.Block())

        @block.sync
        def _(sp):
            sp.dma_start(b1_rows[:], b1.rearrange("e (c p) -> (e c) p", p=P)).then_inc(loaded, 16)
            sp.dma_start(b2_bc[:], b2.rearrange("(a e) d -> a (e d)", a=1).to_broadcast([P, E * D])).then_inc(loaded, 16)
            sp.wait_ge(weights_ready, 1)
            sp.dma_start(x2_dram[:, D:ROW].rearrange("(b p) c -> p b c", p=P), weights[:].bitcast(I32)).then_inc(weights_stored, 16)
            for i in range(2):
                sp.wait_ge(y_scattered[i], 16 * ((TILES + 1 - i) // 2))
            rows = B * P // PARTS
            for i in range(PARTS):
                sp.dma_start(out_rows[i * rows:(i + 1) * rows, :], sum_dram[i * rows:(i + 1) * rows, :]).then_inc(stored, 16)
            sp.wait_ge(stored, 16 * PARTS)

        @block.gpsimd
        def _(pool):
            pool.affine_select(out=below[:], in_=ones[:], compare_op=ALU.is_gt, fill=0.0, base=0,
                               pattern=[[1, P]], channel_multiplier=-1).then_inc(below_ready, 1)
            for k in range(2):
                pool.wait_ge(tile_eq_ready, k + 1)
                pool.tensor_tensor(tile_hot[:, k], tile_hot[:, k], bc(marks[:, k, :], [P, B, TILES], 2), ALU.mult).then_inc(tile_hot_ready, 1)

            def column(dst, ids, i, done):
                pool.wait_ge(ids_ready, 1)
                pool.tensor_copy(dst[:], ids[:, bass.ds(i, 1)]).then_inc(done, 1)
                pool.wait_ge(done, i + 1)
                if not isinstance(i, int):
                    pool.tensor_tensor(spare[:], ones[:, 0:1], ones[:, 0:1], ALU.mult)

            pool.wait_ge(ids_ready, 1)
            for i in range(2):
                pool.wait_ge(x2_stored[i], 16 * (B // 2))
            pool.wait_ge(weights_stored, 16)
            pool.wait_ge(sum_stored, 16 * (B + 1))

            def step(i, par, _):
                if within(i + 3):
                    t = i + 3
                    tp = 1 - par
                    if not isinstance(i, int) or t >= 2:
                        pool.wait_ge(dve_weight, count(t - 2, 2))
                    column(tile_tokens[tp], token_ids, t, pool_tokens)
                    pool.indirect_dma_start(out=xg[tp][:], out_offset=None, in_=x2_dram,
                                            in_offset=bass.IndirectOffsetOnAxis(ap=tile_tokens[tp][:], axis=0)).then_inc(x_gathered[tp], 16)
                if within(i):
                    if not isinstance(i, int) or i >= 1:
                        pool.wait_ge(y_scattered[1 - par], shared(i - 1, 1 - par))
                    pool.wait_ge(dve_y, i + 1)
                    column(tile_rows[par], row_ids, i, pool_rows)
                    pool.indirect_dma_start(out=sum_dram, out_offset=bass.IndirectOffsetOnAxis(ap=tile_rows[par][:], axis=0),
                                            in_=y[par][:], in_offset=None, compute_op=ALU.add).then_inc(y_scattered[par], 16)

            run_tiles(pool, step)

        @block.scalar
        def _(act):
            act.wait_ge(shifted, 1)
            act.activation(prob[:], prob[:], ACT.Exp).then_inc(exp_ready, 1)
            act.activation(spare_act[:], ones[:, 0:1], ACT.Gelu_apprx_tanh)
            act.wait_ge(table_ready, 3)
            act.wait_ge(b1_ready, 1)

            def step(i, par, at):
                if not within(i + 1):
                    return
                t = i + 1
                for k in range(2):
                    act.wait_ge(pe_h, count(t, 2, k + 1))
                    for c in range(4):
                        f = 4 * k + c
                        last = act.activation(h[1 - par][:, f * P:(f + 1) * P], h_bank[2 * (1 - par) + k][:, c * P:(c + 1) * P],
                                              ACT.Gelu_apprx_tanh, bias=b1T[:, bass.ds(at[1] + f, 1)], scale=1.0 / (XS * WS))
                    last.then_inc(act_h, 1)

            run_tiles(act, step, mybir.EngineType.Activation, b1_at, (E - 1) * FC)

        @block.vector
        def _(dve):
            n = [0]

            def chain(ins):
                n[0] += 1
                ins.then_inc(routed, 1)
                dve.wait_ge(routed, n[0])

            full = [P, B, E]
            chain(dve.tensor_reduce(top[:], logits[:], AX.X, ALU.max))
            dve.tensor_tensor(prob[:], logits[:], bc(top[:], full, 2), ALU.subtract).then_inc(shifted, 1)
            dve.wait_ge(exp_ready, 1)
            chain(dve.tensor_reduce(norm[:], prob[:], AX.X, ALU.add))
            chain(dve.reciprocal(norm[:], norm[:]))
            chain(dve.tensor_tensor(prob[:], prob[:], bc(norm[:], full, 2), ALU.mult))
            experts_iota = iota_f[:, 0:E].rearrange("p (a e) -> p a e", a=1).to_broadcast(full)

            def best(p, value, mask):
                chain(dve.tensor_reduce(value[:], p[:], AX.X, ALU.max))
                chain(dve.tensor_tensor(cand[:], p[:], bc(value[:], full, 2), ALU.is_equal))
                chain(dve.scalar_tensor_tensor(cand[:], cand[:], -float(E), experts_iota, ALU.mult, ALU.add))
                chain(dve.tensor_reduce(norm[:], cand[:], AX.X, ALU.min))
                chain(dve.tensor_tensor(mask[:], cand[:], bc(norm[:], full, 2), ALU.is_equal))

            best(prob, top1, first)
            chain(dve.scalar_tensor_tensor(prob2[:], first[:], -2.0, prob[:], ALU.mult, ALU.add))
            best(prob2, top2, second)
            dve.tensor_tensor(chosen[:], first[:], second[:], ALU.add).then_inc(ranks_in, 1)
            chain(dve.tensor_tensor(norm[:], top1[:], top2[:], ALU.add))
            chain(dve.reciprocal(norm[:], norm[:]))
            dve.tensor_tensor(weights[:, :, 0], top1[:], norm[:], ALU.mult)
            dve.tensor_tensor(weights[:, :, 1], top2[:], norm[:], ALU.mult).then_inc(weights_ready, 1)
            dve.wait_ge(pe_b1, 1)
            dve.tensor_copy(b1T[:], h_bank[0][:, 0:E * FC]).then_inc(b1_ready, 1)
            dve.wait_ge(ranks_ready, 1)
            ranks = r_bank[:, 0:P].rearrange("p (b e) -> p b e", e=E)
            thresholds = iota_f[:, 0:KT].rearrange("p (a k) -> p a k", a=1).to_broadcast([P, E, KT])
            chain(dve.tensor_scalar(load[:], r_bank[:, P:P + E], 1.0 / P, None, ALU.mult))
            chain(dve.tensor_tensor(over[:], bc(load[:], [P, E, KT], 2), thresholds, ALU.is_gt))
            chain(dve.tensor_reduce(tiles[:], over[:], AX.X, ALU.add))
            chain(dve.tensor_tensor(earlier[:], bc(tiles[:], [P, E, E], 1), lower[:], ALU.mult))
            chain(dve.tensor_reduce(starts[:], earlier[:], AX.X, ALU.add))
            chain(dve.scalar_tensor_tensor(slot_of[:], bc(starts[:], full, 1), float(P), ranks, ALU.mult, ALU.add))
            for mask, part in ((first, cand), (second, prob2)):
                dve.tensor_tensor(part[:], mask[:], slot_of[:], ALU.mult).then_inc(routed, 1)
                n[0] += 1
            dve.wait_ge(routed, n[0])
            dve.tensor_reduce(slot_f[:, 0, :], cand[:], AX.X, ALU.add)
            chain(dve.tensor_reduce(slot_f[:, 1, :], prob2[:], AX.X, ALU.add))
            chain(dve.tensor_copy(slot_i[:], slot_f[:]))
            chain(dve.tensor_scalar(place_i[:], slot_i[:], P - 1, None, ALU.bitwise_and))
            chain(dve.tensor_copy(place[:], place_i[:]))
            by_tile = [P, B, TILES]
            columns = tile_first[:].rearrange("p (a t) -> p a t", a=1).to_broadcast(by_tile)
            chain(dve.tensor_tensor(tile_start[:], slot_f[:], place[:], ALU.subtract))
            for k in range(2):
                dve.tensor_tensor(tile_hot[:, k], columns, bc(tile_start[:, k, :], by_tile, 2), ALU.is_equal).then_inc(tile_eq_ready, 1)
            for k in range(2):
                for b in range(B):
                    dve.tensor_scalar(place_hot[:, k, b, :], iota_16[:], place[:, k, b:b + 1], None,
                                      ALU.is_equal).then_inc(place_hot_ready, 1)
            dve.wait_ge(marks_in, 1)
            chain(dve.tensor_copy(slot_mark[:], y_bank[1][:, 0:TILES]))
            dve.scalar_tensor_tensor(slot_pad[:], slot_mark[:], 0.0, pad_row[:].to_broadcast([P, TILES]), ALU.is_equal, ALU.mult)
            chain(dve.scalar_tensor_tensor(slot_token[:], slot_mark[:], -1.0, slot_mark[:], ALU.mult, ALU.max))
            chain(dve.tensor_scalar(slot_token[:], slot_token[:], 1.0, -1.0, ALU.max, ALU.add))
            dve.tensor_copy(token_ids[:], slot_token[:]).then_inc(ids_ready, 1)
            chain(dve.tensor_tensor(slot_row[:], slot_token[:], slot_pad[:], ALU.add))
            dve.tensor_copy(row_ids[:], slot_row[:])
            dve.tensor_scalar(is_choice[0][:], slot_mark[:], 0.0, None, ALU.is_gt)
            chain(dve.tensor_scalar(is_choice[1][:], slot_mark[:], 0.0, None, ALU.is_lt))
            chain(dve.tensor_tensor(ends[:], starts[:], tiles[:], ALU.add))
            chain(dve.tensor_tensor(past[:], ends[0:1, :].rearrange("p (a e) -> p a e", a=1).to_broadcast([1, TILES + 1, E]),
                                    iota_f[0:1, 0:TILES + 1].rearrange("p (t a) -> p t a", a=1).to_broadcast([1, TILES + 1, E]), ALU.is_le))
            chain(dve.tensor_reduce(tile_f[:], past[:], AX.X, ALU.add))
            for at, size in ((w_at, DC * F), (b1_at, FC), (b2_at, D)):
                dve.tensor_scalar(at[:], tile_f[:], float(E - 1), float(size), ALU.min, ALU.mult).then_inc(table_ready, 1)
            dve.wait_ge(loaded, 32)
            dve.wait_ge(table_ready, 3)

            def step(i, par, at):
                def split(t, tp, k):
                    half = slice(k * 512, (k + 1) * 512)
                    dve.wait_ge(act_h, count(t, 2, k + 1))
                    dve.tensor_scalar(hh[tp][:, half], h[tp][:, half], XS, None, ALU.mult).then_inc(dve_hi, 1)
                    dve.wait_ge(dve_hi, count(t, 2, k + 1))
                    dve.scalar_tensor_tensor(hl[tp][:, half], h[tp][:, half], XS, hh[tp][:, half],
                                             ALU.mult, ALU.subtract).then_inc(dve_lo, 1)

                if within(i):
                    split(i, par, 1)
                if within(i + 2):
                    t = i + 2
                    dve.wait_ge(pe_x, t + 1)
                    dve.tensor_copy(xgT[par][:], x_bank[:, 0:2 * D].rearrange("p (c t) -> p c t", t=P)).then_inc(dve_x, 1)
                    pair = xg[par][:, D:ROW].bitcast(F32)
                    this = slot_weight[:, bass.ds(t, 1)]
                    dve.tensor_scalar(this, pair[:, 0:1], is_choice[0][:, bass.ds(t, 1)], None, ALU.mult).then_inc(dve_weight, 1)
                    dve.wait_ge(dve_weight, count(t, 2, 1))
                    dve.scalar_tensor_tensor(this, pair[:, 1:2], is_choice[1][:, bass.ds(t, 1)], this, ALU.mult, ALU.add).then_inc(dve_weight, 1)
                if within(i + 1):
                    split(i + 1, 1 - par, 0)
                if within(i):
                    dve.wait_ge(pe_y, i + 1)
                    if not isinstance(i, int) or i >= 2:
                        dve.wait_ge(y_scattered[par], shared(i - 2, par))
                    dve.scalar_tensor_tensor(y[par][:], y_bank[par][:, 0:D], 1.0 / (XS * WS), b2_bc[:, bass.ds(at[0], D)],
                                             ALU.mult, ALU.add).then_inc(dve_yb, 1)
                    dve.wait_ge(dve_yb, i + 1)
                    dve.tensor_scalar(y[par][:], y[par][:], slot_weight[:, bass.ds(i, 1)], None, ALU.mult).then_inc(dve_y, 1)

            run_tiles(dve, step, mybir.EngineType.DVE, b2_at, (E - 1) * D)

        @block.tensor
        def _(pe):
            pe.wait_ge(loaded, 32)
            pe.transpose(h_bank[0][:, 0:E * FC], b1_rows[:], ident[0:E * FC, 0:E * FC]).then_inc(pe_b1, 1)
            pe.wait_ge(below_ready, 1)
            pe.wait_ge(ranks_in, 1)
            flat = chosen[:].rearrange("p b e -> p (b e)")
            pe.matmul(r_bank[:, 0:P], below[:], flat, start=True, stop=False)
            for b in range(B - 1):
                after = bc(chosen[:, b, :], [P, B - 1 - b, E], 1)
                pe.matmul(r_bank[:, (b + 1) * E:P].rearrange("p (b e) -> p b e", e=E), ones[:], after, start=False, stop=(b == B - 2))
            for b in range(B):
                last = pe.matmul(r_bank[:, P:P + E], ones[:], chosen[:, b, :], start=(b == 0), stop=(b == B - 1))
            last.then_inc(ranks_ready, 1)
            for k in range(2):
                pe.wait_ge(tile_hot_ready, k + 1)
                for b in range(B):
                    pe.wait_ge(place_hot_ready, k * B + b + 1)
                    last = pe.matmul(y_bank[1][:, 0:TILES], place_hot[:, k, b, :], tile_hot[:, k, b, :],
                                     start=(k == 0 and b == 0), stop=(k == 1 and b == B - 1))
            last.then_inc(marks_in, 1)
            pe.wait_ge(ids_ready, 1)
            pe.wait_ge(b1_ready, 1)
            pe.wait_ge(table_ready, 3)

            def step(i, par, at):
                t, tp = i + 1, 1 - par
                if within(i):
                    pe.wait_ge(dve_lo, count(i, 2, 1))
                elif within(t):
                    pe.wait_ge(dve_x, t + 1)
                for f in range(FC):
                    k, c = divmod(f, 4)
                    if within(t):
                        terms = [(w, x, d) for d in range(DC) for w, x in ((w1h, 0), (w1h, DC), (w1l, 0))]
                        for m, (w, x, d) in enumerate(terms):
                            last = pe.matmul(h_bank[2 * tp + k][:, c * P:(c + 1) * P],
                                             w[:, bass.ds(at[1] + (d * F + f * P), P)], xgT[tp][:, x + d, :],
                                             start=(m == 0), stop=(m == len(terms) - 1))
                        if c == 3:
                            last.then_inc(pe_h, 1)
                    if f == 3 and within(i + 2):
                        pe.wait_ge(x_gathered[par], shared(i + 2, par))
                        for n in range(2 * DC):
                            last = pe.transpose(x_bank[:, n * P:(n + 1) * P], xg[par][:, n * (P // 2):(n + 1) * (P // 2)].bitcast(F16), ident16[:])
                        last.then_inc(pe_x, 1)
                    if within(i):
                        if f == 4:
                            pe.wait_ge(dve_lo, count(i, 2, 2))
                        for m, (a, w) in enumerate(((hh, w2h), (hl, w2h), (hh, w2l))):
                            last = pe.matmul(y_bank[par][:, 0:D], a[par][:, f * P:(f + 1) * P],
                                             w[:, bass.ds(at[0] + f * D, D)],
                                             start=(f == 0 and m == 0), stop=(f == FC - 1 and m == 2))
                if within(i):
                    last.then_inc(pe_y, 1)

            run_tiles(pe, step, mybir.EngineType.PE, w_at, (E - 1) * DC * F)


_INS = ['x', 'ctx_1024', 'fside_BxSx2_0', 'L0_xattn_Wq', 'L0_xattn_Wkv', 'L0_xattn_Wout', 'L0_xattn_bout',
        'L0_ffn_gate_w', 'L0_ffn_gate_b', 'L0_ffn_w1', 'L0_ffn_b1', 'L0_ffn_w2', 'L0_ffn_b2']
_OUTS = [((16, 128, 256), 'float32')]


def kernel(**inputs):
    import numpy as _np
    import concourse.bacc as _bacc
    from concourse import mybir as _mybir
    from concourse.bass_utils import run_bass_kernel_spmd as _run

    nc = _bacc.Bacc("TRN2", target_bir_lowering=False, num_devices=1)
    arrays, args = {}, []
    for name in _INS:
        a = _np.ascontiguousarray(inputs[name])
        arrays[f"in_{name}_dram"] = a
        args.append(nc.dram_tensor(f"in_{name}_dram", a.shape, _mybir.dt.from_np(a.dtype), kind="ExternalInput").ap())
    for i, (shape, dtype) in enumerate(_OUTS):
        dt = _mybir.dt.from_np(_np.dtype(dtype))
        args.append(nc.dram_tensor(f"out_{i}_dram", shape, dt, kind="ExternalOutput").ap())
    build(nc, *args)
    r = _run(nc, [arrays], core_ids=[0])
    got = tuple(r.results[0][f"out_{i}_dram"] for i in range(len(_OUTS)))
    return got[0]
```
